# Optimizing a Trainium2 kernel written in Bass

```python
import numpy as np
import jax
import jax.numpy as jnp

def _softmax(x, axis=-1):
    return jax.nn.softmax(x, axis=axis)

def _gelu(x):
    return jax.nn.gelu(x, approximate=True)

def _silu(x):
    return jax.nn.silu(x)

def _sigmoid(x):
    return jax.nn.sigmoid(x)

def _layernorm(x, axis=-1, eps=1e-05):
    m = jnp.mean(x, axis=axis, keepdims=True)
    v = jnp.var(x, axis=axis, keepdims=True)
    return (x - m) / jnp.sqrt(v + eps)

def _scatter_add(tgt, idx, src, axis=0):
    return tgt.at[idx].add(src)

def _segment_sum(src, seg, n):
    return jax.ops.segment_sum(src, seg, n)
kernel_name = 'mk_adaln_d1_jaxref_r8_68e664'

def setup_inputs(seed: int=0):
    np.random.seed(seed)
    _w = jnp.asarray

    def _L0_attn_setup():
        import jax, jax.numpy as jnp
        import numpy as np
        N_HEADS = 16
        HIDDEN = 128
        HEAD_DIM = 64
        BSZ = 4
        SEQ = 128
        SCALE = HEAD_DIM ** (-0.5)
        key = jax.random.key(seed)
        k_x, k_q, k_k, k_v, k_o = jax.random.split(key, 5)
        s = HIDDEN ** (-0.5)
        return {'x': jax.random.normal(k_x, (BSZ, SEQ, HIDDEN), dtype=jnp.float32), 'wq': jax.random.normal(k_q, (N_HEADS * HEAD_DIM, HIDDEN), dtype=jnp.float32) * s, 'wk': jax.random.normal(k_k, (N_HEADS * HEAD_DIM, HIDDEN), dtype=jnp.float32) * s, 'wv': jax.random.normal(k_v, (N_HEADS * HEAD_DIM, HIDDEN), dtype=jnp.float32) * s, 'wo': jax.random.normal(k_o, (HIDDEN, N_HEADS * HEAD_DIM), dtype=jnp.float32) * s}
    _L0_attn_in = _L0_attn_setup()

    def _L0_ffn_setup():
        import jax, jax.numpy as jnp
        import numpy as np
        NUM_EXPERTS = 8
        TOP_K = 2
        ROUTE_SCALE = 1.0
        DIM = 128
        HID = 128
        B, S = (2, 512)
        key = jax.random.key(seed)
        ks = jax.random.split(key, 9)
        sc = 0.05
        return {'x': jax.random.normal(ks[0], (B, S, DIM), dtype=jnp.float32), 'gate_w': jax.random.normal(ks[1], (NUM_EXPERTS, DIM), dtype=jnp.float32) * sc, 'w1': jax.random.normal(ks[2], (NUM_EXPERTS, HID, DIM), dtype=jnp.float32) * sc, 'w2': jax.random.normal(ks[3], (NUM_EXPERTS, DIM, HID), dtype=jnp.float32) * sc, 'w3': jax.random.normal(ks[4], (NUM_EXPERTS, HID, DIM), dtype=jnp.float32) * sc, 'sw1': jax.random.normal(ks[5], (HID, DIM), dtype=jnp.float32) * sc, 'sw2': jax.random.normal(ks[6], (DIM, HID), dtype=jnp.float32) * sc, 'sw3': jax.random.normal(ks[7], (HID, DIM), dtype=jnp.float32) * sc, 'expert_bias': jnp.zeros((NUM_EXPERTS,), dtype=jnp.float32)}
    _L0_ffn_in = _L0_ffn_setup()
    _L0_c = _w((lambda *s: np.random.randn(*s).astype(np.float32) * 0.05)(1, 128))
    _L0_wmod = _w((lambda *s: np.random.randn(*s).astype(np.float32) * 0.05)(128, 6 * 128) * 128 ** (-0.5))
    _d = {'L0_attn_x': _L0_attn_in['x'], 'L0_attn_wq': _L0_attn_in['wq'], 'L0_attn_wk': _L0_attn_in['wk'], 'L0_attn_wv': _L0_attn_in['wv'], 'L0_attn_wo': _L0_attn_in['wo'], 'L0_ffn_gate_w': _L0_ffn_in['gate_w'], 'L0_ffn_w1': _L0_ffn_in['w1'], 'L0_ffn_w2': _L0_ffn_in['w2'], 'L0_ffn_w3': _L0_ffn_in['w3'], 'L0_ffn_sw1': _L0_ffn_in['sw1'], 'L0_ffn_sw2': _L0_ffn_in['sw2'], 'L0_ffn_sw3': _L0_ffn_in['sw3'], 'L0_ffn_expert_bias': _L0_ffn_in['expert_bias'], 'L0_c': _L0_c, 'L0_wmod': _L0_wmod}
    _x0 = _d['L0_attn_x']
    _d['L0_attn_x'] = jax.random.normal(jax.random.fold_in(jax.random.key(seed), 1), (1, 2048, 128), dtype=_x0.dtype)
    del _x0
    return _d

def reference(L0_attn_x, L0_attn_wq, L0_attn_wk, L0_attn_wv, L0_attn_wo, L0_ffn_gate_w, L0_ffn_w1, L0_ffn_w2, L0_ffn_w3, L0_ffn_sw1, L0_ffn_sw2, L0_ffn_sw3, L0_ffn_expert_bias, L0_c, L0_wmod):

    def _L0_attn_ref(x, wq, wk, wv, wo):
        import jax, jax.numpy as jnp
        import numpy as np
        N_HEADS = 16
        HIDDEN = 128
        HEAD_DIM = 64
        BSZ = 4
        SEQ = 128
        SCALE = HEAD_DIM ** (-0.5)
        bsz, seqlen, _ = x.shape
        xq = jnp.einsum('bsh,oh->bso', x, wq)
        xk = jnp.einsum('bsh,oh->bso', x, wk)
        xv = jnp.einsum('bsh,oh->bso', x, wv)
        xq = xq.reshape(bsz, N_HEADS, seqlen, HEAD_DIM)
        xk = xk.reshape(bsz, N_HEADS, seqlen, HEAD_DIM)
        xv = xv.reshape(bsz, N_HEADS, seqlen, HEAD_DIM)
        scores = jnp.einsum('bhid,bhjd->bhij', xq, xk) * SCALE
        scores = jax.nn.softmax(scores, axis=-1)
        out = jnp.einsum('bhij,bhjd->bhid', scores, xv)
        out = out.reshape(bsz, seqlen, N_HEADS * HEAD_DIM)
        return jnp.einsum('bso,ho->bsh', out, wo)

    def _L0_ffn_ref(x, gate_w, w1, w2, w3, sw1, sw2, sw3, expert_bias):
        import jax, jax.numpy as jnp
        import numpy as np
        NUM_EXPERTS = 8
        TOP_K = 2
        ROUTE_SCALE = 1.0
        DIM = 128
        HID = 128
        B, S = (2, 512)
        bs, slen, dim = x.shape
        xf = x.reshape(-1, dim)
        scores = jax.nn.sigmoid((xf @ gate_w.T).astype(jnp.float32))
        _, sel = jax.lax.top_k(scores + expert_bias[None, :], TOP_K)
        top_scores = jnp.take_along_axis(scores, sel, axis=1) * ROUTE_SCALE
        flat_sel = sel.reshape(-1)
        order = jnp.argsort(flat_sel, stable=True)
        scores_sorted = top_scores.reshape(-1)[order]
        tok_idx = order // TOP_K
        expert_ids = flat_sel[order]
        routed = xf[tok_idx]
        routed = (routed.astype(jnp.float32) * scores_sorted[:, None]).astype(x.dtype)
        out_r = jnp.zeros_like(routed)
        for e in range(NUM_EXPERTS):
            m = (expert_ids == e)[:, None]
            h = jax.nn.silu(routed @ w1[e].T) * (routed @ w3[e].T)
            out_r = out_r + jnp.where(m, h @ w2[e].T, jnp.zeros((), routed.dtype))
        shared = jax.nn.silu(xf @ sw1.T) * (xf @ sw3.T) @ sw2.T
        out_r = (out_r.astype(jnp.float32) * scores_sorted[:, None]).astype(x.dtype)
        out = shared.at[tok_idx].add(out_r)
        return out.reshape(bs, slen, dim)
    x = L0_attn_x
    mod = (_silu(L0_c) @ L0_wmod).reshape(L0_c.shape[0], 6, 1, -1)
    sa, ca, ga, sb, cb, gb = (mod[:, 0], mod[:, 1], mod[:, 2], mod[:, 3], mod[:, 4], mod[:, 5])
    ga = (2 * (ga >= 0) - 1) * jnp.maximum(jnp.abs(ga), 0.25)
    gb = (2 * (gb >= 0) - 1) * jnp.maximum(jnp.abs(gb), 0.25)
    h = _layernorm(x, axis=-1) * (1 + ca) + sa
    x = x + ga * _L0_attn_ref(h, L0_attn_wq, L0_attn_wk, L0_attn_wv, L0_attn_wo)
    h = _layernorm(x, axis=-1) * (1 + cb) + sb
    x = x + gb * _L0_ffn_ref(h, L0_ffn_gate_w, L0_ffn_w1, L0_ffn_w2, L0_ffn_w3, L0_ffn_sw1, L0_ffn_sw2, L0_ffn_sw3, L0_ffn_expert_bias)
    return x

_drawn_inputs = setup_inputs


def setup_inputs(seed=0):
    import zlib

    import numpy as np

    out = dict(_drawn_inputs(seed))
    spreads = {'L0_ffn_expert_bias': (0.0, 0.8)}
    factors = {'L0_ffn_gate_w': 6.704,
     'L0_ffn_w1': 5.904,
     'L0_ffn_w2': 5.826,
     'L0_ffn_w3': 5.79,
     'L0_ffn_sw1': 8.0,
     'L0_ffn_sw2': 8.0,
     'L0_ffn_sw3': 8.0}
    for name, (base, spread) in spreads.items():
        noise = np.random.default_rng([zlib.crc32(name.encode()), seed]).standard_normal(out[name].shape)
        drawn = base * np.exp(spread * noise) if base else spread * noise
        out[name] = jnp.asarray(drawn.astype(out[name].dtype))
    for name, factor in factors.items():
        out[name] = (out[name] * factor).astype(out[name].dtype)
    return out
```

```python
from contextlib import ExitStack

import concourse.bass as bass
from concourse import mybir

F32 = mybir.dt.float32
F32R = mybir.dt.float32r
ALU = mybir.AluOpType
ACT = mybir.ActivationFunctionType
AX = mybir.AxisListType

P = 128
TOKENS, DIM = 2048, 128
HEADS, HEAD_DIM = 16, 64
BLOCKS = TOKENS // P
CHUNKS = HEADS
POSITIONS = P * CHUNKS
HALF = POSITIONS // 2
BANK = 512
TILES = CHUNKS
PAIRS = TILES // 2
UNITS = 2 * HEADS
EXPERTS, HID = 8, 128
SCALE = HEAD_DIM ** -0.5
EPS = 1e-5
SHIFT_ROW = 64
PROBS = 8

PV_BANK, SIDE_BANK = 4, 6

PEAKS = 32


LONG_JOBS = (
    {2: ("q", 0), 6: ("q", 1), 10: ("k", 0), 12: ("sum", 0), 14: ("k", 1), 16: ("out", 0), 18: ("k", 2),
     20: ("out", 1), 22: ("k", 3)},
    {2: ("q", 2), 6: ("q", 3), 10: ("v", 0), 12: ("sum", 0), 14: ("v", 1), 16: ("out", 0), 20: ("out", 1)},
)
PEAK_PLACES = 26
PROJECTIONS = [("q", 0), ("q", 1)] + [("k", i) for i in range(4)] + [("q", 2), ("q", 3), ("v", 0), ("v", 1)]


def side_jobs(half, last_unit_jobs=True, project=True, peaks=True):
    places = [[] for _ in range(4 * PAIRS)]
    for place, job in LONG_JOBS[half].items():
        if last_unit_jobs if job[0] in ("sum", "out") else project:
            places[place].append(job)
    if peaks:
        peak = 0
        for place in range(PEAK_PLACES):
            single = lambda p: p in LONG_JOBS[half] or (p - 1) in LONG_JOBS[half]
            singles, done = sum(map(single, range(PEAK_PLACES))), sum(map(single, range(place + 1)))
            upto = done + -(-(PEAKS - singles) * (place + 1 - done) // (PEAK_PLACES - singles))
            places[place][:0] = [("peak", i) for i in range(peak, upto)]
            peak = upto
        places[4 * (PAIRS - 1)].append(("shift", 0))
    return [places[4 * step:4 * step + 4] for step in range(PAIRS)]


def build(nc, x, wq, wk, wv, wo, gate_w, w1, w2, w3, sw1, sw2, sw3, expert_bias, cond, wmod, out):
    with ExitStack() as ctx:
        def sb(name, shape, dt=F32):
            return ctx.enter_context(nc.sbuf_tensor(name, shape, dt))

        def sem(name):
            return ctx.enter_context(nc.semaphore(name))

        x_in = sb("x_in", [P, BLOCKS, DIM])
        x_mid = sb("x_mid", [P, BLOCKS, DIM])
        hT = sb("hT", [P, TOKENS])
        h_head = sb("h_head", [P, P])
        wq2 = sb("wq2", [P, CHUNKS, P])
        wk2 = sb("wk2", [P, CHUNKS, P])
        wvT = sb("wvT", [P, CHUNKS * HEAD_DIM])
        wo2 = sb("wo2", [P, CHUNKS, DIM])
        q_hi = sb("q_hi", [P, 2, POSITIONS], F32R)
        q_lo = sb("q_lo", [P, 2, POSITIONS], F32R)
        k_hi_lo = sb("k_hi_lo", [P, 2, POSITIONS], F32R)
        k_shift = sb("k_shift", [P, 2, POSITIONS], F32R)
        v_sb = sb("v_sb", [P, 2, CHUNKS * HEAD_DIM])
        probs = sb("probs", [P, PROBS, HALF])
        acc = sb("acc", [P, 2, HALF])
        oT = sb("oT", [P, HALF])
        w1T = sb("w1T", [P, EXPERTS + 1, HID])
        w3T = sb("w3T", [P, EXPERTS + 1, HID])
        w2T = sb("w2T", [P, EXPERTS + 1, DIM])
        ident = sb("ident", [P, P])
        ones = sb("ones", [P, P])
        shift_mul = sb("shift_mul", [P, 1])
        shift_add = sb("shift_add", [P, 1])
        eps = sb("eps", [P, 1])
        stats = sb("stats", [P, BLOCKS, 6])
        mean_var = sb("mean_var", [P, BLOCKS, 2])
        std = sb("std", [P, BLOCKS])
        rstd = sb("rstd", [P, BLOCKS])
        cond_c = sb("cond_c", [P, 4])
        mod = sb("mod", [P, 6])
        mod_t = sb("mod_t", [P, 4, 2])
        peak_parts = sb("peak_parts", [P, PEAKS])
        peak = sb("peak", [P, 8])
        shift_sb = sb("shift_sb", [8, 2, P], F32R)
        inv_sum = sb("inv_sum", [P, 2, 8])
        y_parts = sb("y_parts", [P, CHUNKS, DIM])
        gateT = sb("gateT", [P, EXPERTS])
        gate_nat = sb("gate_nat", [EXPERTS, DIM])
        bias_row = sb("bias_row", [1, EXPERTS])
        bias_sb = sb("bias_sb", [P, EXPERTS])
        earlier = sb("earlier", [P, EXPERTS, EXPERTS])
        ps = ctx.enter_context(nc.psum_tensor("ps", [P, 8, BANK], F32))

        wq_nat, wk_nat, wv_nat, wmod_nat = (probs[:, i, :] for i in range(4))
        wo_nat = probs[:, 4:6, :].rearrange("p a (c d) -> p (a c) d", d=P)
        w1_nat, w3_nat = (probs[:, 6 + i, :].rearrange("p (e d) -> p e d", d=P) for i in range(2))
        w2_nat = oT[:, :].rearrange("p (e d) -> p e d", d=P)
        sw1_nat, sw3_nat, sw2_nat = (acc[:, 0, i * P:(i + 1) * P] for i in range(3))

        x_loaded, cond_loaded, wmod_loaded = sem("x_loaded"), sem("cond_loaded"), sem("wmod_loaded")
        w_loaded = {n: sem(n + "_loaded") for n in ("wq", "wk", "wv", "wo", "ffn", "small")}
        consts = sem("consts")
        cond_exp, mod_ready, mod_psum = sem("cond_exp"), sem("mod_ready"), sem("mod_psum")
        ln_step, std_ready = sem("ln_step"), sem("std_ready")
        normed = sem("normed")
        folded = sem("folded")
        turned = sem("turned")
        kept_dve, kept_act = sem("kept_dve"), sem("kept_act")
        dve_chain = sem("dve_chain")
        head_copied = sem("head_copied")
        side_full = sem("side_full")
        side_free = [sem("side_free0"), sem("side_free1")]
        hi_ready = sem("hi_ready")
        k_shift_ready = sem("k_shift_ready")
        peak_ready = sem("peak_ready")
        shift_ready = sem("shift_ready")
        scored, exped, pv_done, o_copied = sem("scored"), sem("exped"), sem("pv_done"), sem("o_copied")
        added = sem("added")
        tree, mid_ready = sem("tree"), sem("mid_ready")
        stored = [sem("stored0"), sem("stored1")]

        block = ctx.enter_context(nc.Block())

        FULL_JOBS = sum(len(p) for f in (0, 1) for s in side_jobs(f) for p in s)
        PROLOGUE_JOBS = 10 + PEAKS + 1
        FIRST_MISSING = 3
        STEADY_BASE = PROLOGUE_JOBS - FIRST_MISSING

        def job_number(t, local):
            if isinstance(t, int) and t == 0:
                return PROLOGUE_JOBS + local
            return t * (2 * FULL_JOBS) + (STEADY_BASE + local)

        def bank_of(t, local):
            return (PROLOGUE_JOBS + local) % 2 if isinstance(t, int) and t == 0 else (STEADY_BASE + local) % 2

        def bank_turn(t, local):
            if isinstance(t, int) and t == 0:
                return (PROLOGUE_JOBS + local) // 2
            return t * FULL_JOBS + (STEADY_BASE + local) // 2

        class Job:

            def __init__(self, t, local):
                self.bank = bank_of(t, local) if t is not None else local % 2
                self.turn = bank_turn(t, local) if t is not None else local // 2
                self.full = (job_number(t, local) if t is not None else local) + 1
                self.has_earlier = t is not None or local >= 2
                self.ps = ps[:, SIDE_BANK + self.bank, :]
                self.free = side_free[self.bank]

        def adds(kt):
            return max(1, kt)

        def pairs_of_heads(eng, body):
            state = body(0, None)
            with eng.Fori(1, HEADS // 2 - 1) as t:
                body(t, state)
            body(HEADS // 2 - 1, state)

        def units(t):
            first, last = (isinstance(t, int) and t == 0), (isinstance(t, int) and t == HEADS // 2 - 1)
            for p in (0, 1):
                for half in (0, 1):
                    final_head = last and p == 1
                    plan = side_jobs(half, last_unit_jobs=not (first and p == 0 and half == 0),
                                     project=not final_head, peaks=not (final_head and half == 1))
                    yield p, half, t * 2 + p, t * 4 + (2 * p + half), plan

        PROLOGUE = PROJECTIONS[:6] + [("peak", i) for i in range(PEAKS)] + [("shift", 0)] + PROJECTIONS[6:]
        EPILOGUE = [("sum", 0), ("out", 0), ("out", 1)]
        END_T = HEADS // 2 - 1
        LAST_LOCAL = sum(len(pl) for _, _, _, _, plan in units(END_T) for s in plan for pl in s)

        SETUP = [("wq", 0), ("wq", 1), ("wk", 0), ("wk", 1), ("wv", 0), ("wv", 1)] \
            + [("h", i) for i in range(4)] + [("wo", i) for i in range(4)] \
            + [(n, i) for n in ("w1", "w3", "w2") for i in range(3)] + [("gate", 0)]


        def setup_copies(name, i, src):
            by = lambda s, d: s.rearrange("p (c d) -> p c d", d=d)
            if name in ("wq", "wk"):
                w = wq2 if name == "wq" else wk2
                return [(w[:, 8 * i:8 * i + 8, k * HEAD_DIM:(k + 1) * HEAD_DIM], by(src, HEAD_DIM)) for k in (0, 1)]
            if name == "wv":
                return [(wvT[:, i * BANK:(i + 1) * BANK], src)]
            if name == "wo":
                return [(wo2[:, 4 * i:4 * i + 4, :], by(src, DIM))]
            if name == "gate":
                return [(gateT[:, :], src[:, 0:EXPERTS])]
            w = {"w1": w1T, "w3": w3T, "w2": w2T}[name]
            return [(w[:, 3 * i:3 * i + 3, :], by(src[:, 0:3 * P], P))]

        def layernorm(dve, link, src, dst, nth):
            for b in range(BLOCKS):
                ins = dve.bn_stats(stats[:, b, :], src[:, b, :])
            link(ins)
            for b in range(BLOCKS):
                ins = dve.bn_aggr(mean_var[:, b, :], stats[:, b, :])
            ins.then_inc(ln_step, 1)
            dve.wait_ge(std_ready, nth + 1)
            link(dve.reciprocal(rstd[:, :], std[:, :]))
            for b in range(BLOCKS):
                dve.tensor_scalar(dst[:, b, :], src[:, b, :], mean_var[:, b, 0:1], rstd[:, b:b + 1],
                                  ALU.subtract, ALU.mult).then_inc(normed, 1)

        GROUPS = TOKENS // BANK
        ALL = EXPERTS + 1

        def two(buf):
            return [buf[:, 0:BANK], buf[:, BANK:2 * BANK]]

        weighted = two(probs[:, 0, :])
        silu_sb = two(probs[:, 1, :])
        inner = two(probs[:, 2, :])
        inner_w = two(probs[:, 3, :])
        x_out = two(probs[:, 4, :])
        greater = probs[:, 5, :].rearrange("p (b e j) -> p b e j", e=EXPERTS, j=EXPERTS)
        equal = probs[:, 6, :].rearrange("p (b e j) -> p b e j", e=EXPERTS, j=EXPERTS)
        small = probs[:, 7, :].rearrange("p (n b e) -> p n b e", n=8, e=EXPERTS)
        gate_exp, gate_den, score, biased, rank, chosen = (small[:, n] for n in range(6))
        LOW_ROW = 32
        weight_nat = sb("weight_nat", [P, BLOCKS, LOW_ROW + EXPERTS])
        weight_hi = sb("weight_hi", [P, BLOCKS, EXPERTS], F32R)
        weightT = q_hi[0:LOW_ROW + EXPERTS, 0, :]
        select = k_hi_lo[0:LOW_ROW + EXPERTS, 0, 0:EXPERTS * P].rearrange("p (e m) -> p e m", m=P)

        logits = sem("logits")
        gate_exped = sem("gate_exped")
        weights_ready = sem("weights_ready")
        turned2, kept2_act, kept2_dve = sem("turned2"), sem("kept2_act"), sem("kept2_dve")
        bcast = sem("bcast")
        weighted_ready = sem("weighted_ready")
        ups, silued, inner_ready, inner_w_ready = sem("ups"), sem("silued"), sem("inner_ready"), sem("inner_w_ready")
        downs, out_ready = sem("downs"), sem("out_ready")

        def banks(m):
            return ps[:, m % 2, :], ps[:, 2 + m % 2, :], ps[:, 4 + m % 2, :]

        def routed(m):
            return m // ALL * EXPERTS + min(m % ALL, EXPERTS)

        ITEMS = GROUPS * ALL

        def ffn_pe(pe):
            for i in range(4):
                for k in range(4):
                    pe.wait_ge(normed, BLOCKS + 4 * i + k + 1)
                    mm = pe.transpose(ps[:, i, k * P:(k + 1) * P], x_in[:, 4 * i + k, :], ident[:, :])
                mm.then_inc(turned2, 1)
            pe.wait_ge(w_loaded["small"], 32)
            pe.matmul(ps[:, 5, 0:EXPERTS], ones[0:1, :], bias_row[:, :], start=True, stop=True)
            for b in range(BLOCKS):
                if b % 4 == 0:
                    pe.wait_ge(kept2_dve if b % 8 == 0 else kept2_act, b // 8 + 1)
                mm = pe.matmul(ps[:, 4, b * EXPERTS:(b + 1) * EXPERTS], hT[:, b * P:(b + 1) * P], gateT[:, :],
                               start=True, stop=True)
            mm.then_inc(logits, 1)
            for i in range(4):
                pe.wait_ge(weights_ready, 1)
                for k in range(4):
                    mm = pe.transpose(ps[0:LOW_ROW + EXPERTS, i, k * P:(k + 1) * P], weight_nat[:, 4 * i + k, :],
                                      ident[:, :])
                mm.then_inc(turned2, 1)

            def spread(m):
                if m % ALL == EXPERTS:
                    return
                g, e = m // ALL, m % ALL
                if m >= 2:
                    pe.wait_ge(inner_w_ready, m - 1)
                pe.matmul(banks(m)[0], select[:, e, :], weightT[:, g * BANK:(g + 1) * BANK],
                          start=True, stop=True).then_inc(bcast, 1)

            def down(m):
                g, e = m // ALL, m % ALL
                if e == 0 and g >= 2:
                    pe.wait_ge(out_ready, g - 1)
                pe.wait_ge(inner_w_ready, m + 1)
                for k in range(4):
                    mm = pe.matmul(ps[:, 6 + g % 2, k * P:(k + 1) * P], inner_w[m % 2][:, k * P:(k + 1) * P],
                                   w2T[:, e, :], start=(e == 0 and k == 0), stop=(e == ALL - 1 and k == 3),
                                   skip_group_check=True)
                mm.then_inc(downs, 1)

            pe.wait_ge(kept2_dve, 5)
            pe.wait_ge(kept2_act, 4)
            spread(0)
            for m in range(ITEMS):
                g, e = m // ALL, m % ALL
                if m + 1 < ITEMS:
                    spread(m + 1)
                rhs = hT[:, g * BANK:(g + 1) * BANK] if e == EXPERTS else weighted[m % 2]
                if e < EXPERTS:
                    pe.wait_ge(weighted_ready, routed(m) + 1)
                if m >= 2:
                    pe.wait_ge(inner_ready, m - 1)
                pe.matmul(banks(m)[1], w1T[:, e, :], rhs, start=True, stop=True)
                pe.matmul(banks(m)[2], w3T[:, e, :], rhs, start=True, stop=True).then_inc(ups, 1)
                if m >= 1:
                    down(m - 1)
            down(ITEMS - 1)

        def ffn_act(act):
            act.wait_ge(ln_step, 2)
            act.activation(std[:, :], mean_var[:, :, 1], ACT.Sqrt, bias=eps[:, :]).then_inc(std_ready, 1)
            for i in (1, 3):
                act.wait_ge(turned2, i + 1)
                act.activation(hT[:, i * BANK:(i + 1) * BANK], ps[:, i, :], ACT.Identity, scale=mod[:, 4:5],
                               bias=mod[:, 3:4]).then_inc(kept2_act, 1)
            act.wait_ge(logits, 1)
            act.activation(gate_exp, ps[:, 4, 0:BLOCKS * EXPERTS].rearrange("p (b e) -> p b e", e=EXPERTS), ACT.Exp,
                           scale=-1.0).then_inc(gate_exped, 1)
            for i in (1, 3):
                act.wait_ge(turned2, 4 + i + 1)
                act.copy(weightT[:, i * BANK:(i + 1) * BANK],
                         ps[0:LOW_ROW + EXPERTS, i, :]).then_inc(kept2_act, 1)
            for m in range(ITEMS):
                act.wait_ge(ups, m + 1)
                if m >= 2:
                    act.wait_ge(inner_ready, m - 1)
                act.activation(silu_sb[m % 2], banks(m)[1], ACT.Silu).then_inc(silued, 1)

        def ffn_dve(dve, link):
            dve.wait_ge(mid_ready, HEADS)
            layernorm(dve, link, x_mid, x_in, 1)
            for i in (0, 2):
                dve.wait_ge(turned2, i + 1)
                dve.tensor_scalar(hT[:, i * BANK:(i + 1) * BANK], ps[:, i, :], mod[:, 4:5], mod[:, 3:4],
                                  ALU.mult, ALU.add).then_inc(kept2_dve, 1)
            dve.wait_ge(logits, 1)
            n = LOW_ROW + EXPERTS
            dve.tensor_tensor(select, ident[0:n, 0:EXPERTS, None].broadcast_to([n, EXPERTS, P]),
                              ident[0:n, LOW_ROW:n, None].broadcast_to([n, EXPERTS, P]), ALU.add).then_inc(kept2_dve, 1)
            dve.memset(weight_nat[:, :, :], 0.0).then_inc(logits, 1)
            dve.tensor_copy(bias_sb[:, :], ps[:, 5, 0:EXPERTS]).then_inc(logits, 1)
            dve.wait_ge(gate_exped, 1)
            link(dve.tensor_scalar(gate_den, gate_exp, 1.0, None, ALU.add))
            link(dve.reciprocal(score, gate_den))
            dve.wait_ge(logits, 3)
            link(dve.tensor_tensor(biased, score, bias_sb[:, None, :].broadcast_to([P, BLOCKS, EXPERTS]), ALU.add))
            mine = biased[:, :, :, None].broadcast_to([P, BLOCKS, EXPERTS, EXPERTS])
            other = biased[:, :, None, :].broadcast_to([P, BLOCKS, EXPERTS, EXPERTS])
            dve.wait_ge(consts, 7 + EXPERTS - 1)
            dve.tensor_tensor(greater, other, mine, ALU.is_gt)
            link(dve.tensor_tensor(equal, other, mine, ALU.is_equal))
            link(dve.tensor_tensor(equal, equal, earlier[:, None, :, :].broadcast_to(
                [P, BLOCKS, EXPERTS, EXPERTS]), ALU.mult))
            link(dve.tensor_tensor(greater, greater, equal, ALU.add))
            link(dve.tensor_reduce(rank, greater, AX.X, ALU.add))
            link(dve.tensor_scalar(chosen, rank, 1.5, None, ALU.is_lt))
            link(dve.tensor_tensor(gate_den, chosen, score, ALU.mult))
            link(dve.tensor_copy(weight_hi[:, :, :], gate_den))
            dve.tensor_copy(weight_nat[:, :, 0:EXPERTS], weight_hi[:, :, :])
            dve.tensor_tensor(weight_nat[:, :, LOW_ROW:n], gate_den, weight_hi[:, :, :],
                              ALU.subtract).then_inc(weights_ready, 1)
            for i in (0, 2):
                dve.wait_ge(turned2, 4 + i + 1)
                dve.tensor_copy(weightT[:, i * BANK:(i + 1) * BANK],
                                ps[0:n, i, :]).then_inc(kept2_dve, 1)

            def weigh_tokens(m):
                g, e = m // ALL, m % ALL
                if e == EXPERTS:
                    return
                dve.wait_ge(bcast, routed(m) + 1)
                if m >= 2:
                    dve.wait_ge(ups, m - 1)
                dve.tensor_tensor(weighted[m % 2], hT[:, g * BANK:(g + 1) * BANK], banks(m)[0],
                                  ALU.mult).then_inc(weighted_ready, 1)

            weigh_tokens(0)
            for m in range(ITEMS):
                g, e = m // ALL, m % ALL
                if m + 1 < ITEMS:
                    weigh_tokens(m + 1)
                dve.wait_ge(silued, m + 1)
                if m >= 2:
                    dve.wait_ge(downs, m - 1)
                if e == EXPERTS:
                    dve.tensor_tensor(inner_w[m % 2], silu_sb[m % 2], banks(m)[2], ALU.mult).then_inc(inner_ready, 1)
                    dve.wait_ge(inner_ready, m + 1)
                    dve.engine_nop().then_inc(inner_w_ready, 1)
                else:
                    dve.tensor_tensor(inner[m % 2], silu_sb[m % 2], banks(m)[2], ALU.mult).then_inc(inner_ready, 1)
                    dve.wait_ge(inner_ready, m + 1)
                    dve.tensor_tensor(inner_w[m % 2], inner[m % 2], banks(m)[0], ALU.mult).then_inc(inner_w_ready, 1)
                if e == ALL - 1:
                    dve.wait_ge(downs, m + 1)
                    if g >= 2:
                        dve.wait_ge(stored[g % 2], 16 * (g // 2))
                    dve.tensor_tensor(x_out[g % 2].rearrange("p (b d) -> p b d", d=DIM),
                                      ps[:, 6 + g % 2, :].rearrange("p (b d) -> p b d", d=DIM),
                                      x_mid[:, 4 * g:4 * g + 4, :], ALU.add).then_inc(out_ready, 1)

        def ffn_store(sp):
            for g in range(GROUPS):
                sp.wait_ge(out_ready, g + 1)
                sp.dma_start(out[0, g * BANK:(g + 1) * BANK, :].rearrange("(b p) d -> p b d", p=P),
                             x_out[g % 2].rearrange("p (b d) -> p b d", d=DIM)).then_inc(stored[g % 2], 16)
            for n in (0, 1):
                sp.wait_ge(stored[n], 16 * (GROUPS // 2))

        @block.sync
        def _(sp):
            sp.dma_start(x_in[:, 0:8, :], x[0, 0:1024, :].rearrange("(b p) d -> p b d", p=P)).then_inc(x_loaded, 16)
            sp.dma_start(wq_nat.rearrange("p (b d) -> p b d", d=DIM),
                         wq.rearrange("(b p) d -> p b d", p=P)).then_inc(w_loaded["wq"], 16)
            sp.dma_start(wk_nat.rearrange("p (b d) -> p b d", d=DIM),
                         wk.rearrange("(b p) d -> p b d", p=P)).then_inc(w_loaded["wk"], 16)
            sp.dma_start(wv_nat.rearrange("p (b d) -> p b d", d=DIM),
                         wv.rearrange("(b p) d -> p b d", p=P)).then_inc(w_loaded["wv"], 16)
            wo_c = wo.rearrange("h (c d) -> h c d", d=HEAD_DIM)
            sp.dma_start(wo_nat[:, :, 0:HEAD_DIM], wo_c).then_inc(w_loaded["wo"], 16)
            sp.dma_start(wo_nat[:, :, HEAD_DIM:P], wo_c).then_inc(w_loaded["wo"], 16)
            sp.dma_start(w1_nat, w1.rearrange("e f d -> f e d")).then_inc(w_loaded["ffn"], 16)
            sp.dma_start(w3_nat, w3.rearrange("e f d -> f e d")).then_inc(w_loaded["ffn"], 16)
            sp.dma_start(w2_nat, w2.rearrange("e d f -> d e f")).then_inc(w_loaded["ffn"], 16)
            sp.dma_start(sw1_nat, sw1).then_inc(w_loaded["ffn"], 16)
            sp.dma_start(sw3_nat, sw3).then_inc(w_loaded["ffn"], 16)
            sp.dma_start(sw2_nat, sw2).then_inc(w_loaded["ffn"], 16)

            def send_shift(job, target_parity, target_half):
                sp.wait_ge(job.free, job.turn + 1)
                sp.dma_start(
                    q_lo[SHIFT_ROW:SHIFT_ROW + 1, target_parity,
                         target_half * HALF:(target_half + 1) * HALF].bitcast(F32),
                    shift_sb[:, target_half, :].bitcast(F32),
                ).then_inc(shift_ready, 16)

            send_shift(Job(None, PROLOGUE.index(("shift", 0))), 0, 0)

            def body(t, _):
                local = 0
                for p, half, head, unit, plan in units(t):
                    for places in plan:
                        for jobs in places:
                            for kind, i in jobs:
                                if kind == "shift":
                                    send_shift(Job(t, local), p if half == 0 else 1 - p, 1 - half)
                                local += 1

            pairs_of_heads(sp, body)
            ffn_store(sp)

        @block.scalar
        def _(act):
            act.dma_start(cond_c[:, 0:1], cond.rearrange("a d -> d a")).then_inc(cond_loaded, 16)
            act.dma_start(wmod_nat[:, 0:768], wmod).then_inc(wmod_loaded, 16)
            act.dma_start(x_in[:, 8:16, :], x[0, 1024:2048, :].rearrange("(b p) d -> p b d", p=P)).then_inc(x_loaded, 16)
            act.dma_start(gate_nat[:, :], gate_w).then_inc(w_loaded["small"], 16)
            act.dma_start(bias_row[:, :], expert_bias.rearrange("(a e) -> a e", a=1)).then_inc(w_loaded["small"], 16)
            act.wait_ge(cond_loaded, 16)
            act.activation(cond_c[:, 1:2], cond_c[:, 0:1], ACT.Exp, scale=-1.0).then_inc(cond_exp, 1)
            act.wait_ge(consts, 4)
            act.wait_ge(ln_step, 1)
            act.activation(std[:, :], mean_var[:, :, 1], ACT.Sqrt, bias=eps[:, :]).then_inc(std_ready, 1)

            for n, (name, i) in enumerate(SETUP):
                if n % 2 == 0:
                    continue
                act.wait_ge(turned, n + 1)
                src = ps[:, n % 8, :]
                if name == "h":
                    act.wait_ge(mod_ready, 1)
                    act.activation(hT[:, i * BANK:(i + 1) * BANK], src, ACT.Identity, scale=mod[:, 1:2],
                                   bias=mod[:, 0:1]).then_inc(kept_act, 1)
                else:
                    for dst, s in setup_copies(name, i, src)[:-1]:
                        act.copy(dst, s)
                    dst, s = setup_copies(name, i, src)[-1]
                    act.copy(dst, s).then_inc(kept_act, 1)

            def side(job, kind, i, parity):
                cols = slice(i * BANK, (i + 1) * BANK)
                if kind in "qk":
                    act.wait_ge(side_full, job.full)
                    hi = q_hi if kind == "q" else k_hi_lo
                    act.copy(hi[:, parity, cols], job.ps).then_inc(hi_ready, 1)
                if kind == "v":
                    act.wait_ge(side_full, job.full)
                    act.copy(v_sb[:, parity, cols], job.ps).then_inc(job.free, 1)

            def put_shift_factor(job, n, parity):
                act.wait_ge(job.free, job.turn + 1)
                cols = slice(n * HALF, (n + 1) * HALF)
                act.activation(k_shift[:, parity, cols], k_hi_lo[:, parity, cols], ACT.Identity,
                               scale=shift_mul[:, 0:1], bias=shift_add[:, 0:1]).then_inc(k_shift_ready, 1)

            def copy_head(head):
                if isinstance(head, int):
                    act.copy(h_head[:, :], hT[:, head * P:(head + 1) * P]).then_inc(head_copied, 1)
                else:
                    act.copy(h_head[:, :], hT[:, bass.ds(head * P, P)]).then_inc(head_copied, 1)

            def copy_pv(unit_done):
                act.wait_ge(pv_done, PAIRS * unit_done)
                act.copy(oT[:, :], ps[:, PV_BANK:PV_BANK + 2, :].rearrange("p a b -> p (a b)")).then_inc(o_copied, 1)

            act.wait_ge(kept_dve, 5)
            act.wait_ge(kept_act, 5)
            copy_head(0)
            for local, (kind, i) in enumerate(PROLOGUE):
                side(Job(None, local), kind, i, 0)
                if kind == "k" and i % 2:
                    act.wait_ge(consts, 6)
                    put_shift_factor(Job(None, local), i // 2, 0)

            def body(t, _):
                local = 0
                k_jobs = {}
                for p, half, head, unit, plan in units(t):
                    first = isinstance(t, int) and t == 0 and p == 0 and half == 0
                    last_head = isinstance(t, int) and t == END_T and p == 1
                    if half == 0 and not last_head:
                        copy_head(head + 1)
                    for step, places in enumerate(plan):
                        for place, jobs in enumerate(places):
                            if place < 2:
                                kt = 2 * step + place
                                act.wait_ge(scored, unit * TILES + (kt + 1))
                                if not (first and kt < PROBS):
                                    old = kt - PROBS
                                    if kt % 2 == 0:
                                        act.wait_ge(pv_done, unit * PAIRS + (old // 2 + 1))
                                    act.wait_ge(added, unit * (TILES - 1) + (adds(old % TILES)
                                                - (TILES - 1 if old < 0 else 0)))
                                act.activation(probs[:, kt % PROBS, :],
                                               ps[:, 2 * place:2 * place + 2, :].rearrange("p a b -> p (a b)"),
                                               ACT.Exp, scale=SCALE).then_inc(exped, 1)
                            for kind, i in jobs:
                                if kind == "k":
                                    k_jobs[i] = Job(t, local)
                                side(Job(t, local), kind, i, 1 - p)
                                local += 1
                            if step == PAIRS - 1 and place < 2 and half == 0 and not last_head:
                                put_shift_factor(k_jobs[2 * place + 1], place, 1 - p)
                        if step == 0 and not first:
                            copy_pv(unit)

            pairs_of_heads(act, body)
            copy_pv(UNITS)
            ffn_act(act)

        @block.gpsimd
        def _(pool):
            pool.memset(ident[:, :], 0.0).then_inc(consts, 1)
            pool.memset(ones[:, :], 1.0).then_inc(consts, 1)
            pool.wait_ge(consts, 2)
            pool.affine_select(out=ident[:, :], in_=ident[:, :], compare_op=ALU.not_equal, fill=1.0, base=0,
                               pattern=[[-1, P]], channel_multiplier=1).then_inc(consts, 1)
            pool.memset(eps[:, :], EPS).then_inc(consts, 1)
            pool.wait_ge(consts, 3)
            row = ident[:, SHIFT_ROW:SHIFT_ROW + 1]
            pool.tensor_scalar(shift_mul[:, :], row, -1.0, 1.0, ALU.mult, ALU.add).then_inc(consts, 1)
            pool.tensor_scalar(shift_add[:, :], row, -1.0, None, ALU.mult).then_inc(consts, 1)
            pool.memset(earlier[:, :, :], 0.0).then_inc(consts, 1)
            pool.wait_ge(consts, 7)
            for e in range(1, EXPERTS):
                pool.memset(earlier[:, e, 0:e], 1.0).then_inc(consts, 1)

            def add_tile(unit, half, kt):
                pool.wait_ge(exped, unit * TILES + (kt + 1))
                total = acc[:, half, :]
                if kt > 1:
                    pool.wait_ge(added, unit * (TILES - 1) + (kt - 1))
                pool.tensor_tensor(total, total if kt > 1 else probs[:, 0, :], probs[:, kt % PROBS, :],
                                   ALU.add).then_inc(added, 1)

            def sum_head(job, head):
                pool.wait_ge(job.free, job.turn + 1)
                for k, n in enumerate((8, 4, 2, 1)):
                    pool.tensor_tensor(y_parts[:, 0:n, :], y_parts[:, 0:n, :], y_parts[:, n:2 * n, :],
                                       ALU.add).then_inc(tree, 1)
                    pool.wait_ge(tree, head * 4 + (k + 1))
                at = slice(head, head + 1) if isinstance(head, int) else bass.ds(head, 1)
                pool.tensor_tensor(x_mid[:, at, :], y_parts[:, 0:1, :], x_in[:, at, :], ALU.add).then_inc(mid_ready, 1)

            def body(t, _):
                local = 0
                for p, half, head, unit, plan in units(t):
                    first = isinstance(t, int) and t == 0 and p == 0 and half == 0
                    for step, places in enumerate(plan):
                        for place, jobs in enumerate(places):
                            kt = 2 * step + place
                            if 0 < kt < 2 * step + 2:
                                add_tile(unit, half, kt)
                            for kind, i in jobs:
                                if kind == "out" and i == 1 and half == 0 and not first:
                                    sum_head(Job(t, local), head - 1)
                                local += 1

            pairs_of_heads(pool, body)
            sum_head(Job(END_T, LAST_LOCAL + 2), HEADS - 1)

        @block.vector
        def _(dve):
            links = [0]

            def link(ins):
                links[0] += 1
                ins.then_inc(dve_chain, 1)
                dve.wait_ge(dve_chain, links[0])

            dve.wait_ge(cond_exp, 1)
            link(dve.tensor_scalar(cond_c[:, 2:3], cond_c[:, 1:2], 1.0, None, ALU.add))
            link(dve.reciprocal(cond_c[:, 3:4], cond_c[:, 2:3]))
            dve.tensor_tensor(cond_c[:, 1:2], cond_c[:, 0:1], cond_c[:, 3:4], ALU.mult).then_inc(mod_psum, 1)
            dve.wait_ge(x_loaded, 32)
            layernorm(dve, link, x_in, x_mid, 0)
            dve.wait_ge(mod_psum, 2)
            link(dve.tensor_copy(mod[:, :], ps[:, 7, 0:6]))
            gates = mod[:, 2:6:3]
            link(dve.tensor_scalar(mod_t[:, 0, :], gates, 0.0, None, ALU.is_ge))
            link(dve.tensor_scalar(mod_t[:, 1, :], mod_t[:, 0, :], 2.0, -1.0, ALU.mult, ALU.add))
            link(dve.tensor_tensor(mod_t[:, 2, :], mod_t[:, 1, :], gates, ALU.mult))
            link(dve.tensor_scalar(mod_t[:, 3, :], mod_t[:, 2, :], 0.25, None, ALU.max))
            link(dve.tensor_tensor(gates, mod_t[:, 3, :], mod_t[:, 1, :], ALU.mult))
            link(dve.tensor_scalar(mod[:, 1:5:3], mod[:, 1:5:3], 1.0, None, ALU.add))
            dve.wait_ge(w_loaded["wo"], 32)
            dve.tensor_scalar(wo_nat, wo_nat, mod[:, 2:3], None, ALU.mult).then_inc(mod_ready, 1)
            dve.wait_ge(w_loaded["ffn"], 96)
            dve.tensor_scalar(w2_nat, w2_nat, mod[:, 5:6], None, ALU.mult).then_inc(folded, 1)
            dve.tensor_scalar(sw2_nat, sw2_nat, mod[:, 5:6], None, ALU.mult).then_inc(folded, 1)
            for n, (name, i) in enumerate(SETUP):
                if n % 2:
                    continue
                dve.wait_ge(turned, n + 1)
                src = ps[:, n % 8, :]
                if name == "h":
                    dve.tensor_scalar(hT[:, i * BANK:(i + 1) * BANK], src, mod[:, 1:2], mod[:, 0:1],
                                      ALU.mult, ALU.add).then_inc(kept_dve, 1)
                else:
                    for dst, s in setup_copies(name, i, src)[:-1]:
                        dve.tensor_copy(dst, s)
                    dst, s = setup_copies(name, i, src)[-1]
                    dve.tensor_copy(dst, s).then_inc(kept_dve, 1)

            def side(job, kind, i, target_unit, target_half, high, parity, head_before, last_half):
                if kind == "v":
                    return
                dve.wait_ge(side_full, job.full)
                cols = slice(i * BANK, (i + 1) * BANK)
                if kind == "q":
                    dve.wait_ge(hi_ready, high)
                    dve.tensor_tensor(q_lo[:, parity, cols], job.ps, q_hi[:, parity, cols],
                                      ALU.subtract).then_inc(job.free, 1)
                if kind == "k":
                    dve.wait_ge(hi_ready, high)
                    low = k_hi_lo[HEAD_DIM:P, parity, cols]
                    dve.tensor_tensor(low, job.ps[HEAD_DIM:P, :], low, ALU.subtract).then_inc(job.free, 1)
                if kind == "peak":
                    dve.tensor_reduce(peak_parts[:, i:i + 1], job.ps, AX.X, ALU.max).then_inc(job.free, 1)
                    if i == PEAKS - 1:
                        dve.wait_ge(job.free, job.turn + 1)
                        dve.wait_ge(side_free[1 - job.bank], job.turn + job.bank)
                        dve.tensor_reduce(peak[:, :], peak_parts[:, :].rearrange("p (c b) -> p c b", b=4),
                                          AX.X, ALU.max).then_inc(peak_ready, 1)
                if kind == "shift":
                    if not (isinstance(target_unit, int) and target_unit < 2):
                        dve.wait_ge(shift_ready, target_unit * 16 - 16)
                    dve.tensor_copy(shift_sb[:, target_half, :], job.ps[0:8, 0:P]).then_inc(job.free, 1)
                if kind == "sum":
                    dve.reciprocal(inv_sum[:, last_half, :], job.ps[:, 0:8]).then_inc(job.free, 1)
                    dve.wait_ge(job.free, job.turn + 1)
                if kind == "out":
                    if i == 0 and last_half == 0 and not (isinstance(head_before, int) and head_before == 0):
                        dve.wait_ge(mid_ready, head_before)
                    chunk = 8 * last_half + 4 * i
                    dve.tensor_tensor(y_parts[:, chunk:chunk + 4, :], job.ps.rearrange("p (c d) -> p c d", d=DIM),
                                      inv_sum[:, last_half, 4 * i:4 * i + 4, None].broadcast_to([P, 4, DIM]),
                                      ALU.mult).then_inc(job.free, 1)

            for local, (kind, i) in enumerate(PROLOGUE):
                high = PROJECTIONS.index((kind, i)) + 1 if kind in "qk" else 0
                side(Job(None, local), kind, i, 0, 0, high, 0, None, None)

            def body(t, _):
                local = 0
                for p, half, head, unit, plan in units(t):
                    for places in plan:
                        for jobs in places:
                            for kind, i in jobs:
                                high = head * 8 + (8 + PROJECTIONS.index((kind, i)) + 1 if kind in "qk" else 0)
                                side(Job(t, local), kind, i, unit + 1, 1 - half, high, 1 - p, head - 1 + half,
                                     1 - half)
                                local += 1

            pairs_of_heads(dve, body)
            for k, (kind, i) in enumerate(EPILOGUE):
                job = Job(END_T, LAST_LOCAL + k)
                side(job, kind, i, None, None, None, None, HEADS - 1, 1)
            ffn_dve(dve, link)

        @block.tensor
        def _(pe):
            pe.wait_ge(mod_psum, 1)
            pe.wait_ge(wmod_loaded, 16)
            for i in range(6):
                mm = pe.matmul(ps[:, 7, i:i + 1], wmod_nat[:, i * P:(i + 1) * P], cond_c[:, 1:2], start=True, stop=True)
            mm.then_inc(mod_psum, 1)
            pe.wait_ge(consts, 3)
            for n, (name, i) in enumerate(SETUP):
                if n == 7:
                    pe.wait_ge(mod_ready, 1)
                if n >= 8:
                    pe.wait_ge(kept_act if n % 2 else kept_dve, (n - 8) // 2 + 1)
                bank = ps[:, n % 8, :]
                if name in ("wq", "wk", "wv"):
                    pe.wait_ge(w_loaded[name], 16)
                    nat = {"wq": wq_nat, "wk": wk_nat, "wv": wv_nat}[name]
                    for k in range(4):
                        mm = pe.transpose(bank[:, k * P:(k + 1) * P], nat[:, (4 * i + k) * P:(4 * i + k + 1) * P],
                                          ident[:, :])
                if name == "h":
                    for k in range(4):
                        pe.wait_ge(normed, 4 * i + k + 1)
                        mm = pe.transpose(bank[:, k * P:(k + 1) * P], x_mid[:, 4 * i + k, :], ident[:, :])
                if name == "wo":
                    pe.wait_ge(mod_ready, 1)
                    for k in range(4):
                        mm = pe.transpose(bank[:, k * P:(k + 1) * P], wo_nat[:, 4 * i + k, :], ident[:, :])
                if name in ("w1", "w2", "w3"):
                    if name == "w1" and i == 0:
                        pe.wait_ge(w_loaded["ffn"], 96)
                        pe.wait_ge(folded, 2)
                    nat, shared = {"w1": (w1_nat, sw1_nat), "w2": (w2_nat, sw2_nat), "w3": (w3_nat, sw3_nat)}[name]
                    for k in range(3):
                        e = 3 * i + k
                        mm = pe.transpose(bank[:, k * P:(k + 1) * P], nat[:, e, :] if e < EXPERTS else shared,
                                          ident[:, :])
                if name == "gate":
                    pe.wait_ge(w_loaded["small"], 32)
                    mm = pe.transpose(bank[:, 0:EXPERTS], gate_nat[:, :], ident[0:EXPERTS, 0:EXPERTS])
                mm.then_inc(turned, 1)

            def side(job, kind, i, parity, target_parity, target_half, target_unit, heads_copied,
                     before_unit, last_half):
                if job.has_earlier:
                    pe.wait_ge(job.free, job.turn)
                bank = job.ps
                if kind in "qk":
                    if kind == "q" and i == 0:
                        pe.wait_ge(head_copied, heads_copied)
                    w = wq2 if kind == "q" else wk2
                    for k in range(4):
                        mm = pe.matmul(bank[:, k * P:(k + 1) * P], w[:, 4 * i + k, :], h_head[:, :],
                                       start=True, stop=True)
                if kind == "v":
                    mm = pe.matmul(bank, h_head[:, :], wvT[:, i * BANK:(i + 1) * BANK], start=True, stop=True)
                if kind == "peak":
                    q = target_half * HALF + (i // 4) * P
                    mm = pe.matmul(bank, q_hi[:, target_parity, q:q + P],
                                   k_hi_lo[:, target_parity, (i % 4) * BANK:(i % 4 + 1) * BANK], start=True, stop=True)
                if kind == "shift":
                    pe.wait_ge(peak_ready, target_unit + 1)
                    mm = pe.transpose(bank[0:8, 0:P], peak[:, :], ident[:, :])
                if kind == "sum":
                    pe.wait_ge(added, before_unit * (TILES - 1) + (TILES - 1))
                    for c in range(8):
                        mm = pe.matmul(bank[:, c:c + 1], acc[:, last_half, c * P:(c + 1) * P], ones[:, 0:1],
                                       start=True, stop=True)
                if kind == "out":
                    if i == 0:
                        pe.wait_ge(o_copied, before_unit + 1)
                    for k in range(4):
                        c = 4 * i + k
                        mm = pe.matmul(bank[:, k * P:(k + 1) * P], oT[:, c * P:(c + 1) * P],
                                       wo2[:, 8 * last_half + c, :], start=True, stop=True)
                mm.then_inc(side_full, 1)

            def scores(p, half, head, unit, kt):
                slot = 2 * (kt % 2)
                q = half * HALF
                first = isinstance(unit, int) and unit == 0
                if not (first and kt < 2):
                    pe.wait_ge(exped, unit * TILES + (kt - 1))
                for b in range(2):
                    pe.matmul(ps[:, slot + b, :], k_hi_lo[:, p, kt * P:(kt + 1) * P],
                              q_hi[:, p, q + b * BANK:q + (b + 1) * BANK], start=True, stop=False)
                if kt == 0:
                    if half == 0:
                        pe.wait_ge(k_shift_ready, head * 2 + 2)
                    pe.wait_ge(shift_ready, unit * 16 + 16)
                for b in range(2):
                    mm = pe.matmul(ps[:, slot + b, :], k_shift[:, p, kt * P:(kt + 1) * P],
                                   q_lo[:, p, q + b * BANK:q + (b + 1) * BANK], start=False, stop=True)
                mm.then_inc(scored, 1)

            def weigh(p, unit, pair, b):
                if b == 0:
                    if not (isinstance(unit, int) and unit == 0) and pair == 0:
                        pe.wait_ge(o_copied, unit)
                    pe.wait_ge(exped, unit * TILES + (2 * pair + 2))
                for k in range(2):
                    kt = 2 * pair + k
                    at = HEAD_DIM * k
                    mm = pe.matmul(ps[at:at + HEAD_DIM, PV_BANK + b, :], v_sb[:, p, kt * HEAD_DIM:(kt + 1) * HEAD_DIM],
                                   probs[:, kt % PROBS, b * BANK:(b + 1) * BANK],
                                   start=(pair == 0), stop=(pair == PAIRS - 1), tile_position=(0, at))
                if b == 1:
                    mm.then_inc(pv_done, 1)

            pe.wait_ge(kept_act, len(SETUP) // 2)
            pe.wait_ge(kept_dve, (len(SETUP) + 1) // 2)
            for local, (kind, i) in enumerate(PROLOGUE):
                side(Job(None, local), kind, i, 0, 0, 0, 0, 1, None, None)

            def body(t, _):
                local = 0
                for p, half, head, unit, plan in units(t):
                    first = isinstance(t, int) and t == 0 and p == 0 and half == 0
                    for step, places in enumerate(plan):
                        for place, jobs in enumerate(places):
                            if place < 2:
                                scores(p, half, head, unit, 2 * step + place)
                            elif step > 0:
                                weigh(p, unit, step - 1, place - 2)
                            elif not first:
                                weigh(p if half else 1 - p, unit - 1, PAIRS - 1, place - 2)
                            for kind, i in jobs:
                                side(Job(t, local), kind, i, 1 - p, p if half == 0 else 1 - p, 1 - half, unit + 1,
                                     head + 2, unit - 1, 1 - half)
                                local += 1

            pairs_of_heads(pe, body)
            for b in range(2):
                weigh(1, UNITS - 1, PAIRS - 1, b)
            for k, (kind, i) in enumerate(EPILOGUE):
                side(Job(END_T, LAST_LOCAL + k), kind, i, None, None, None, None, None, UNITS - 1, 1)
            ffn_pe(pe)


_INS = ['L0_attn_x', 'L0_attn_wq', 'L0_attn_wk', 'L0_attn_wv', 'L0_attn_wo', 'L0_ffn_gate_w', 'L0_ffn_w1',
        'L0_ffn_w2', 'L0_ffn_w3', 'L0_ffn_sw1', 'L0_ffn_sw2', 'L0_ffn_sw3', 'L0_ffn_expert_bias', 'L0_c', 'L0_wmod']
_OUTS = [((1, TOKENS, DIM), 'float32')]


def kernel(**inputs):
    import numpy as _np
    import concourse.bacc as _bacc
    from concourse import mybir as _mybir
    from concourse.bass_utils import run_bass_kernel_spmd as _run

    nc = _bacc.Bacc("TRN2", target_bir_lowering=False, num_devices=1)
    arrays, args = {}, []
    for name in _INS:
        a = _np.ascontiguousarray(inputs[name])
        arrays[f"in_{name}_dram"] = a
        args.append(nc.dram_tensor(f"in_{name}_dram", a.shape, _mybir.dt.from_np(a.dtype), kind="ExternalInput").ap())
    for i, (shape, dtype) in enumerate(_OUTS):
        dt = _mybir.dt.from_np(_np.dtype(dtype))
        args.append(nc.dram_tensor(f"out_{i}_dram", shape, dt, kind="ExternalOutput").ap())
    build(nc, *args)
    r = _run(nc, [arrays], core_ids=[0])
    got = tuple(r.results[0][f"out_{i}_dram"] for i in range(len(_OUTS)))
    return got[0]
```

```python
from contextlib import ExitStack

import concourse.bass as bass
from concourse import mybir

F32 = mybir.dt.float32
F32R = mybir.dt.float32r
ALU = mybir.AluOpType
ACT = mybir.ActivationFunctionType
AX = mybir.AxisListType

P = 128
TOKENS, DIM = 2048, 128
HEADS, HEAD_DIM = 16, 64
BLOCKS = TOKENS // P
CHUNKS = HEADS
POSITIONS = P * CHUNKS
HALF = POSITIONS // 2
BANK = 512
TILES = CHUNKS
PAIRS = TILES // 2
UNITS = 2 * HEADS
EXPERTS, HID = 8, 128
SCALE = HEAD_DIM ** -0.5
EPS = 1e-5
SHIFT_ROW = 64
PROBS = 8

PV_BANK, SIDE_BANK = 4, 6

PEAKS = 32


LONG_JOBS = (
    {2: ("q", 0), 6: ("q", 1), 10: ("k", 0), 12: ("sum", 0), 14: ("k", 1), 16: ("out", 0), 18: ("k", 2),
     20: ("out", 1), 22: ("k", 3)},
    {2: ("q", 2), 6: ("q", 3), 10: ("v", 0), 12: ("sum", 0), 14: ("v", 1), 16: ("out", 0), 20: ("out", 1)},
)
PEAK_PLACES = 26
LAST_UNIT_JOBS = {8: ("turn", 0), 9: ("turn", 1), 10: ("turn", 2), 11: ("logits", 0)}
READY_BLOCKS = 12
PROJECTIONS = [("q", 0), ("q", 1)] + [("k", i) for i in range(4)] + [("q", 2), ("q", 3), ("v", 0), ("v", 1)]


def side_jobs(half, last_unit_jobs=True, project=True, peaks=True, last_unit=False):
    places = [[] for _ in range(4 * PAIRS)]
    for place, job in LONG_JOBS[half].items():
        if last_unit_jobs if job[0] in ("sum", "out") else project:
            places[place].append(job)
    if peaks:
        peak = 0
        for place in range(PEAK_PLACES):
            single = lambda p: p in LONG_JOBS[half] or (p - 1) in LONG_JOBS[half]
            singles, done = sum(map(single, range(PEAK_PLACES))), sum(map(single, range(place + 1)))
            upto = done + -(-(PEAKS - singles) * (place + 1 - done) // (PEAK_PLACES - singles))
            places[place][:0] = [("peak", i) for i in range(peak, upto)]
            peak = upto
        places[4 * (PAIRS - 1)].append(("shift", 0))
    if last_unit:
        for place, job in LAST_UNIT_JOBS.items():
            places[place].append(job)
    return [places[4 * step:4 * step + 4] for step in range(PAIRS)]


def build(nc, x, wq, wk, wv, wo, gate_w, w1, w2, w3, sw1, sw2, sw3, expert_bias, cond, wmod, out):
    with ExitStack() as ctx:
        def sb(name, shape, dt=F32):
            return ctx.enter_context(nc.sbuf_tensor(name, shape, dt))

        def sem(name):
            return ctx.enter_context(nc.semaphore(name))

        x_in = sb("x_in", [P, BLOCKS, DIM])
        x_mid = sb("x_mid", [P, BLOCKS, DIM])
        hT = sb("hT", [P, TOKENS])
        h_head = sb("h_head", [P, P])
        wq2 = sb("wq2", [P, CHUNKS, P])
        wk2 = sb("wk2", [P, CHUNKS, P])
        wvT = sb("wvT", [P, CHUNKS * HEAD_DIM])
        wo2 = sb("wo2", [P, CHUNKS, DIM])
        q_hi = sb("q_hi", [P, 2, POSITIONS], F32R)
        q_lo = sb("q_lo", [P, 2, POSITIONS], F32R)
        k_hi_lo = sb("k_hi_lo", [P, 2, POSITIONS], F32R)
        k_shift = sb("k_shift", [P, 2, POSITIONS], F32R)
        v_sb = sb("v_sb", [P, 2, CHUNKS * HEAD_DIM])
        probs = sb("probs", [P, PROBS, HALF])
        acc = sb("acc", [P, 2, HALF])
        oT = sb("oT", [P, HALF])
        w1T = sb("w1T", [P, EXPERTS + 1, HID])
        w3T = sb("w3T", [P, EXPERTS + 1, HID])
        w2T = sb("w2T", [P, EXPERTS + 1, DIM])
        ident = sb("ident", [P, P])
        ones = sb("ones", [P, P])
        shift_mul = sb("shift_mul", [P, 1])
        shift_add = sb("shift_add", [P, 1])
        eps = sb("eps", [P, 1])
        stats = sb("stats", [P, BLOCKS, 6])
        mean_var = sb("mean_var", [P, BLOCKS, 2])
        std = sb("std", [P, BLOCKS])
        rstd = sb("rstd", [P, BLOCKS])
        cond_c = sb("cond_c", [P, 4])
        mod = sb("mod", [P, 6])
        mod_t = sb("mod_t", [P, 4, 2])
        peak_parts = sb("peak_parts", [P, PEAKS])
        peak = sb("peak", [P, 8])
        shift_sb = sb("shift_sb", [8, 2, P], F32R)
        inv_sum = sb("inv_sum", [P, 2, 8])
        y_parts = sb("y_parts", [P, CHUNKS, DIM])
        gateT = sb("gateT", [P, EXPERTS])
        gate_nat = sb("gate_nat", [EXPERTS, DIM])
        bias_row = sb("bias_row", [1, EXPERTS])
        bias_sb = sb("bias_sb", [P, EXPERTS])
        earlier = sb("earlier", [P, EXPERTS, EXPERTS])
        ps = ctx.enter_context(nc.psum_tensor("ps", [P, 8, BANK], F32))

        wq_nat, wk_nat, wv_nat, wmod_nat = (probs[:, i, :] for i in range(4))
        wo_nat = probs[:, 4:6, :].rearrange("p a (c d) -> p (a c) d", d=P)
        w1_nat, w3_nat = (probs[:, 6 + i, :].rearrange("p (e d) -> p e d", d=P) for i in range(2))
        w2_nat = oT[:, :].rearrange("p (e d) -> p e d", d=P)
        sw1_nat, sw3_nat, sw2_nat = (acc[:, 0, i * P:(i + 1) * P] for i in range(3))

        x_loaded, cond_loaded, wmod_loaded = sem("x_loaded"), sem("cond_loaded"), sem("wmod_loaded")
        w_loaded = {n: sem(n + "_loaded") for n in ("wq", "wk", "wv", "wo", "ffn", "small")}
        consts = sem("consts")
        cond_exp, mod_ready, mod_psum = sem("cond_exp"), sem("mod_ready"), sem("mod_psum")
        ln_step, std_ready = sem("ln_step"), sem("std_ready")
        normed = sem("normed")
        folded = sem("folded")
        turned = sem("turned")
        kept_dve, kept_act = sem("kept_dve"), sem("kept_act")
        dve_chain = sem("dve_chain")
        head_copied = sem("head_copied")
        side_full = sem("side_full")
        side_free = [sem("side_free0"), sem("side_free1")]
        hi_ready = sem("hi_ready")
        k_shift_ready = sem("k_shift_ready")
        peak_ready = sem("peak_ready")
        shift_ready = sem("shift_ready")
        scored, exped, pv_done, o_copied = sem("scored"), sem("exped"), sem("pv_done"), sem("o_copied")
        added = sem("added")
        tree, mid_ready = sem("tree"), sem("mid_ready")
        stored = [sem("stored0"), sem("stored1")]

        block = ctx.enter_context(nc.Block())

        FULL_JOBS = sum(len(p) for f in (0, 1) for s in side_jobs(f) for p in s)
        PROLOGUE_JOBS = 10 + PEAKS + 1
        FIRST_MISSING = 3
        STEADY_BASE = PROLOGUE_JOBS - FIRST_MISSING

        def job_number(t, local):
            if isinstance(t, int) and t == 0:
                return PROLOGUE_JOBS + local
            return t * (2 * FULL_JOBS) + (STEADY_BASE + local)

        def bank_of(t, local):
            return (PROLOGUE_JOBS + local) % 2 if isinstance(t, int) and t == 0 else (STEADY_BASE + local) % 2

        def bank_turn(t, local):
            if isinstance(t, int) and t == 0:
                return (PROLOGUE_JOBS + local) // 2
            return t * FULL_JOBS + (STEADY_BASE + local) // 2

        class Job:

            def __init__(self, t, local):
                self.bank = bank_of(t, local) if t is not None else local % 2
                self.turn = bank_turn(t, local) if t is not None else local // 2
                self.full = (job_number(t, local) if t is not None else local) + 1
                self.has_earlier = t is not None or local >= 2
                self.ps = ps[:, SIDE_BANK + self.bank, :]
                self.free = side_free[self.bank]

        def adds(kt):
            return max(1, kt)

        def pairs_of_heads(eng, body):
            state = body(0, None)
            with eng.Fori(1, HEADS // 2 - 1) as t:
                body(t, state)
            body(HEADS // 2 - 1, state)

        def units(t):
            first, last = (isinstance(t, int) and t == 0), (isinstance(t, int) and t == HEADS // 2 - 1)
            for p in (0, 1):
                for half in (0, 1):
                    final_head = last and p == 1
                    plan = side_jobs(half, last_unit_jobs=not (first and p == 0 and half == 0),
                                     project=not final_head, peaks=not (final_head and half == 1),
                                     last_unit=final_head and half == 1)
                    yield p, half, t * 2 + p, t * 4 + (2 * p + half), plan

        PROLOGUE = PROJECTIONS[:6] + [("peak", i) for i in range(PEAKS)] + [("shift", 0)] + PROJECTIONS[6:]
        EPILOGUE = [("weights", 0), ("weights", 1), ("weights", 2), ("sum", 0), ("out", 0), ("out", 1)]
        END_T = HEADS // 2 - 1
        LAST_LOCAL = sum(len(pl) for _, _, _, _, plan in units(END_T) for s in plan for pl in s)

        ALL_JOBS = job_number(END_T, LAST_LOCAL + len(EPILOGUE))

        class LateJob:

            def __init__(self, n):
                self.bank, self.turn, self.full = 1, ALL_JOBS // 2 + n, ALL_JOBS + n + 1
                self.has_earlier = True
                self.ps = ps[:, SIDE_BANK + 1, :]
                self.free = side_free[1]

        LATE = [("turn", 3), ("logits", 1), ("weights", 3)]

        def gating_blocks(i):
            return range(READY_BLOCKS) if i == 0 else range(READY_BLOCKS, BLOCKS)

        SETUP = [("wq", 0), ("wq", 1), ("wk", 0), ("wk", 1), ("wv", 0), ("wv", 1)] \
            + [("h", i) for i in range(4)] + [("wo", i) for i in range(4)] \
            + [(n, i) for n in ("w1", "w3", "w2") for i in range(3)] + [("gate", 0)]


        def setup_copies(name, i, src):
            by = lambda s, d: s.rearrange("p (c d) -> p c d", d=d)
            if name in ("wq", "wk"):
                w = wq2 if name == "wq" else wk2
                return [(w[:, 8 * i:8 * i + 8, k * HEAD_DIM:(k + 1) * HEAD_DIM], by(src, HEAD_DIM)) for k in (0, 1)]
            if name == "wv":
                return [(wvT[:, i * BANK:(i + 1) * BANK], src)]
            if name == "wo":
                return [(wo2[:, 4 * i:4 * i + 4, :], by(src, DIM))]
            if name == "gate":
                return [(gateT[:, :], src[:, 0:EXPERTS]), (bias_sb[:, :], src[:, EXPERTS:2 * EXPERTS])]
            w = {"w1": w1T, "w3": w3T, "w2": w2T}[name]
            return [(w[:, 3 * i:3 * i + 3, :], by(src[:, 0:3 * P], P))]

        def layernorm_stats(dve, link, src, blocks):
            for b in blocks:
                ins = dve.bn_stats(stats[:, b, :], src[:, b, :])
            link(ins)
            for b in blocks:
                ins = dve.bn_aggr(mean_var[:, b, :], stats[:, b, :])
            ins.then_inc(ln_step, 1)

        def layernorm_apply(dve, link, src, dst, blocks, nth):
            dve.wait_ge(std_ready, nth)
            b0, b1 = blocks[0], blocks[-1] + 1
            link(dve.reciprocal(rstd[:, b0:b1], std[:, b0:b1]))
            for b in blocks:
                dve.tensor_scalar(dst[:, b, :], src[:, b, :], mean_var[:, b, 0:1], rstd[:, b:b + 1],
                                  ALU.subtract, ALU.mult).then_inc(normed, 1)

        def layernorm_root(act, blocks, nth):
            act.wait_ge(ln_step, nth)
            b0, b1 = blocks[0], blocks[-1] + 1
            act.activation(std[:, b0:b1], mean_var[:, b0:b1, 1], ACT.Sqrt, bias=eps[:, :]).then_inc(std_ready, 1)

        GROUPS = TOKENS // BANK
        ALL = EXPERTS + 1

        def two(buf):
            return [buf[:, 0:BANK], buf[:, BANK:2 * BANK]]

        weighted = two(probs[:, 0, :])
        silu_sb = two(probs[:, 1, :])
        inner = two(probs[:, 2, :])
        inner_w = two(probs[:, 3, :])
        x_out = two(probs[:, 4, :])
        greater = wq2[:, 0:8, :].rearrange("p c (e j) -> p (c e j)", j=EXPERTS).rearrange(
            "p (b e j) -> p b e j", e=EXPERTS, j=EXPERTS)
        equal = wq2[:, 8:16, :].rearrange("p c (e j) -> p (c e j)", j=EXPERTS).rearrange(
            "p (b e j) -> p b e j", e=EXPERTS, j=EXPERTS)
        token_weight = [wk2[:, 4 * n:4 * n + 4, :].rearrange("p c d -> p (c d)") for n in range(4)]
        small = wvT[:, :].rearrange("p (n b e) -> p n b e", n=8, e=EXPERTS)
        gate_exp, gate_den, score, biased, rank, chosen = (small[:, n] for n in range(6))
        LOW_ROW = 32
        weight_nat = sb("weight_nat", [P, BLOCKS, LOW_ROW + EXPERTS])
        weight_hi = sb("weight_hi", [P, BLOCKS, EXPERTS], F32R)
        weightT = q_hi[0:LOW_ROW + EXPERTS, 0, :]
        select = k_hi_lo[0:LOW_ROW + EXPERTS, 0, 0:EXPERTS * P].rearrange("p (e m) -> p e m", m=P)

        weights_ready = sem("weights_ready")
        select_ready = sem("select_ready")
        bcast, bcast_kept = sem("bcast"), sem("bcast_kept")
        weighted_ready = sem("weighted_ready")
        ups, silued, inner_ready, inner_w_ready = sem("ups"), sem("silued"), sem("inner_ready"), sem("inner_w_ready")
        downs, out_ready = sem("downs"), sem("out_ready")

        def banks(m):
            return ps[:, 2 + m % 2, :], ps[:, 4 + m % 2, :]

        def routed(m):
            return m // ALL * EXPERTS + min(m % ALL, EXPERTS)

        ITEMS = GROUPS * ALL

        LATE_STATS, LATE_NORM, LATE_GATE = 2, 3, 6
        LATE_AFTER = {4: 0, 5: 1, 8: 2}

        def spread(pe, m):
            if m % ALL == EXPERTS or m >= ITEMS:
                return
            g, e = m // ALL, m % ALL
            if e == 0:
                job = Job(END_T, LAST_LOCAL + EPILOGUE.index(("weights", g))) if g < 3 else LateJob(2)
                pe.wait_ge(job.free, job.turn + 1)
            if m == 0:
                pe.wait_ge(select_ready, 1)
            n = routed(m)
            if n >= 2:
                pe.wait_ge(bcast_kept, n - 1)
            pe.matmul(ps[:, n % 2, :], select[:, e, :], weightT[:, g * BANK:(g + 1) * BANK],
                      start=True, stop=True).then_inc(bcast, 1)

        def keep_spread(act, m):
            if m % ALL == EXPERTS or m >= ITEMS:
                return
            n = routed(m)
            act.wait_ge(bcast, n + 1)
            if n >= 4:
                old = (n - 4) // EXPERTS * ALL + (n - 4) % EXPERTS
                act.wait_ge(inner_w_ready, old + 1)
            act.copy(token_weight[n % 4], ps[:, n % 2, :]).then_inc(bcast_kept, 1)

        def weigh_tokens(pool, m):
            g, e = m // ALL, m % ALL
            if e == EXPERTS:
                return
            n = routed(m)
            pool.wait_ge(bcast_kept, n + 1)
            if m >= 2:
                pool.wait_ge(ups, m - 1)
            pool.tensor_tensor(weighted[m % 2], hT[:, g * BANK:(g + 1) * BANK], token_weight[n % 4],
                               ALU.mult).then_inc(weighted_ready, 1)

        def ffn_pe(pe, side):
            def down(m):
                g, e = m // ALL, m % ALL
                if m == 0:
                    pe.wait_ge(side_free[0], ALL_JOBS - ALL_JOBS // 2)
                if e == 0 and g >= 2:
                    pe.wait_ge(out_ready, g - 1)
                pe.wait_ge(inner_w_ready, m + 1)
                for k in range(4):
                    mm = pe.matmul(ps[:, 6 + g % 2, k * P:(k + 1) * P], inner_w[m % 2][:, k * P:(k + 1) * P],
                                   w2T[:, e, :], start=(e == 0 and k == 0), stop=(e == ALL - 1 and k == 3),
                                   skip_group_check=True)
                mm.then_inc(downs, 1)

            for m in range(ITEMS):
                g, e = m // ALL, m % ALL
                spread(pe, m + 2)
                rhs = hT[:, g * BANK:(g + 1) * BANK] if e == EXPERTS else weighted[m % 2]
                if e < EXPERTS:
                    pe.wait_ge(weighted_ready, routed(m) + 1)
                if m >= 2:
                    pe.wait_ge(inner_ready, m - 1)
                pe.matmul(banks(m)[0], w1T[:, e, :], rhs, start=True, stop=True)
                pe.matmul(banks(m)[1], w3T[:, e, :], rhs, start=True, stop=True).then_inc(ups, 1)
                if m >= 1:
                    down(m - 1)
                if m in LATE_AFTER:
                    side(LateJob(LATE_AFTER[m]), *LATE[LATE_AFTER[m]], None, None, None, None, None, None, None)
            down(ITEMS - 1)

        def gating_act(act, job, kind, i):
            act.wait_ge(side_full, job.full)
            cols = slice(i * BANK, (i + 1) * BANK)
            if kind == "turn":
                act.activation(hT[:, cols], job.ps, ACT.Identity, scale=mod[:, 4:5],
                               bias=mod[:, 3:4]).then_inc(job.free, 1)
            if kind == "logits":
                blocks = gating_blocks(i)
                act.activation(gate_exp[:, blocks[0]:blocks[-1] + 1, :],
                               job.ps[:, 0:len(blocks) * EXPERTS].rearrange("p (b e) -> p b e", e=EXPERTS), ACT.Exp,
                               scale=-1.0).then_inc(job.free, 1)
            if kind == "weights":
                act.copy(weightT[:, cols], job.ps[0:LOW_ROW + EXPERTS, :]).then_inc(job.free, 1)

        def ffn_act(act):
            for m in range(ITEMS):
                keep_spread(act, m + 2)
                act.wait_ge(ups, m + 1)
                if m >= 2:
                    act.wait_ge(inner_ready, m - 1)
                act.activation(silu_sb[m % 2], banks(m)[0], ACT.Silu).then_inc(silued, 1)
                if m == LATE_STATS:
                    layernorm_root(act, range(READY_BLOCKS, BLOCKS), 3)
                if m in LATE_AFTER:
                    gating_act(act, LateJob(LATE_AFTER[m]), *LATE[LATE_AFTER[m]])

        def make_select(dve):
            n = LOW_ROW + EXPERTS
            dve.tensor_tensor(select, ident[0:n, 0:EXPERTS, None].broadcast_to([n, EXPERTS, P]),
                              ident[0:n, LOW_ROW:n, None].broadcast_to([n, EXPERTS, P]),
                              ALU.add).then_inc(select_ready, 1)

        def gate(dve, link, job, i):
            dve.wait_ge(job.free, job.turn + 1)
            blocks = gating_blocks(i)
            at, n = slice(blocks[0], blocks[-1] + 1), len(blocks)
            link(dve.tensor_scalar(gate_den[:, at], gate_exp[:, at], 1.0, None, ALU.add))
            link(dve.reciprocal(score[:, at], gate_den[:, at]))
            link(dve.tensor_tensor(biased[:, at], score[:, at], bias_sb[:, None, :].broadcast_to([P, n, EXPERTS]),
                                   ALU.add))
            mine = biased[:, at, :, None].broadcast_to([P, n, EXPERTS, EXPERTS])
            other = biased[:, at, None, :].broadcast_to([P, n, EXPERTS, EXPERTS])
            dve.tensor_tensor(greater[:, at], other, mine, ALU.is_gt)
            link(dve.tensor_tensor(equal[:, at], other, mine, ALU.is_equal))
            link(dve.tensor_tensor(equal[:, at], equal[:, at], earlier[:, None, :, :].broadcast_to(
                [P, n, EXPERTS, EXPERTS]), ALU.mult))
            link(dve.tensor_tensor(greater[:, at], greater[:, at], equal[:, at], ALU.add))
            link(dve.tensor_reduce(rank[:, at], greater[:, at], AX.X, ALU.add))
            link(dve.tensor_scalar(chosen[:, at], rank[:, at], 1.5, None, ALU.is_lt))
            link(dve.tensor_tensor(gate_den[:, at], chosen[:, at], score[:, at], ALU.mult))
            link(dve.tensor_copy(weight_hi[:, at, :], gate_den[:, at]))
            dve.tensor_copy(weight_nat[:, at, 0:EXPERTS], weight_hi[:, at, :])
            dve.tensor_tensor(weight_nat[:, at, LOW_ROW:LOW_ROW + EXPERTS], gate_den[:, at], weight_hi[:, at, :],
                              ALU.subtract).then_inc(weights_ready, 1)

        def ffn_dve(dve, link):
            def add_up(g):
                dve.wait_ge(downs, ALL * (g + 1))
                if g >= 2:
                    dve.wait_ge(stored[g % 2], 16 * (g // 2))
                dve.tensor_tensor(x_out[g % 2].rearrange("p (b d) -> p b d", d=DIM),
                                  ps[:, 6 + g % 2, :].rearrange("p (b d) -> p b d", d=DIM),
                                  x_mid[:, 4 * g:4 * g + 4, :], ALU.add).then_inc(out_ready, 1)

            for m in range(ITEMS):
                g, e = m // ALL, m % ALL
                dve.wait_ge(silued, m + 1)
                if m >= 2:
                    dve.wait_ge(downs, m - 1)
                if e == EXPERTS:
                    dve.tensor_tensor(inner_w[m % 2], silu_sb[m % 2], banks(m)[1], ALU.mult).then_inc(inner_ready, 1)
                    dve.wait_ge(inner_ready, m + 1)
                    dve.engine_nop().then_inc(inner_w_ready, 1)
                else:
                    dve.tensor_tensor(inner[m % 2], silu_sb[m % 2], banks(m)[1], ALU.mult).then_inc(inner_ready, 1)
                    dve.wait_ge(inner_ready, m + 1)
                    dve.tensor_tensor(inner_w[m % 2], inner[m % 2], token_weight[routed(m) % 4],
                                      ALU.mult).then_inc(inner_w_ready, 1)
                if m == LATE_STATS:
                    dve.wait_ge(mid_ready, HEADS)
                    layernorm_stats(dve, link, x_mid, range(READY_BLOCKS, BLOCKS))
                if m == LATE_NORM:
                    layernorm_apply(dve, link, x_mid, x_in, range(READY_BLOCKS, BLOCKS), 3)
                if m == LATE_GATE:
                    gate(dve, link, LateJob(1), 1)
                if e == 1 and g > 0:
                    add_up(g - 1)
            add_up(GROUPS - 1)

        def ffn_store(sp):
            for g in range(GROUPS):
                sp.wait_ge(out_ready, g + 1)
                sp.dma_start(out[0, g * BANK:(g + 1) * BANK, :].rearrange("(b p) d -> p b d", p=P),
                             x_out[g % 2].rearrange("p (b d) -> p b d", d=DIM)).then_inc(stored[g % 2], 16)
            for n in (0, 1):
                sp.wait_ge(stored[n], 16 * (GROUPS // 2))

        @block.sync
        def _(sp):
            sp.dma_start(x_in[:, 0:8, :], x[0, 0:1024, :].rearrange("(b p) d -> p b d", p=P)).then_inc(x_loaded, 16)
            sp.dma_start(wq_nat.rearrange("p (b d) -> p b d", d=DIM),
                         wq.rearrange("(b p) d -> p b d", p=P)).then_inc(w_loaded["wq"], 16)
            sp.dma_start(wk_nat.rearrange("p (b d) -> p b d", d=DIM),
                         wk.rearrange("(b p) d -> p b d", p=P)).then_inc(w_loaded["wk"], 16)
            sp.dma_start(wv_nat.rearrange("p (b d) -> p b d", d=DIM),
                         wv.rearrange("(b p) d -> p b d", p=P)).then_inc(w_loaded["wv"], 16)
            wo_c = wo.rearrange("h (c d) -> h c d", d=HEAD_DIM)
            sp.dma_start(wo_nat[:, :, 0:HEAD_DIM], wo_c).then_inc(w_loaded["wo"], 16)
            sp.dma_start(wo_nat[:, :, HEAD_DIM:P], wo_c).then_inc(w_loaded["wo"], 16)
            sp.dma_start(w1_nat, w1.rearrange("e f d -> f e d")).then_inc(w_loaded["ffn"], 16)
            sp.dma_start(w3_nat, w3.rearrange("e f d -> f e d")).then_inc(w_loaded["ffn"], 16)
            sp.dma_start(w2_nat, w2.rearrange("e d f -> d e f")).then_inc(w_loaded["ffn"], 16)
            sp.dma_start(sw1_nat, sw1).then_inc(w_loaded["ffn"], 16)
            sp.dma_start(sw3_nat, sw3).then_inc(w_loaded["ffn"], 16)
            sp.dma_start(sw2_nat, sw2).then_inc(w_loaded["ffn"], 16)

            def send_shift(job, target_parity, target_half):
                sp.wait_ge(job.free, job.turn + 1)
                sp.dma_start(
                    q_lo[SHIFT_ROW:SHIFT_ROW + 1, target_parity,
                         target_half * HALF:(target_half + 1) * HALF].bitcast(F32),
                    shift_sb[:, target_half, :].bitcast(F32),
                ).then_inc(shift_ready, 16)

            send_shift(Job(None, PROLOGUE.index(("shift", 0))), 0, 0)

            def body(t, _):
                local = 0
                for p, half, head, unit, plan in units(t):
                    for places in plan:
                        for jobs in places:
                            for kind, i in jobs:
                                if kind == "shift":
                                    send_shift(Job(t, local), p if half == 0 else 1 - p, 1 - half)
                                local += 1

            pairs_of_heads(sp, body)
            ffn_store(sp)

        @block.scalar
        def _(act):
            act.dma_start(cond_c[:, 0:1], cond.rearrange("a d -> d a")).then_inc(cond_loaded, 16)
            act.dma_start(wmod_nat[:, 0:768], wmod).then_inc(wmod_loaded, 16)
            act.dma_start(x_in[:, 8:16, :], x[0, 1024:2048, :].rearrange("(b p) d -> p b d", p=P)).then_inc(x_loaded, 16)
            act.dma_start(gate_nat[:, :], gate_w).then_inc(w_loaded["small"], 16)
            act.dma_start(bias_row[:, :], expert_bias.rearrange("(a e) -> a e", a=1)).then_inc(w_loaded["small"], 16)
            act.wait_ge(cond_loaded, 16)
            act.activation(cond_c[:, 1:2], cond_c[:, 0:1], ACT.Exp, scale=-1.0).then_inc(cond_exp, 1)
            act.wait_ge(consts, 4)
            layernorm_root(act, range(BLOCKS), 1)

            for n, (name, i) in enumerate(SETUP):
                if n % 2 == 0:
                    continue
                act.wait_ge(turned, n + 1)
                src = ps[:, n % 8, :]
                if name == "h":
                    act.wait_ge(mod_ready, 1)
                    act.activation(hT[:, i * BANK:(i + 1) * BANK], src, ACT.Identity, scale=mod[:, 1:2],
                                   bias=mod[:, 0:1]).then_inc(kept_act, 1)
                else:
                    for dst, s in setup_copies(name, i, src)[:-1]:
                        act.copy(dst, s)
                    dst, s = setup_copies(name, i, src)[-1]
                    act.copy(dst, s).then_inc(kept_act, 1)

            def side(job, kind, i, parity):
                cols = slice(i * BANK, (i + 1) * BANK)
                if kind in ("turn", "logits", "weights"):
                    gating_act(act, job, kind, i)
                if kind in ("q", "k"):
                    act.wait_ge(side_full, job.full)
                    hi = q_hi if kind == "q" else k_hi_lo
                    act.copy(hi[:, parity, cols], job.ps).then_inc(hi_ready, 1)
                if kind == "v":
                    act.wait_ge(side_full, job.full)
                    act.copy(v_sb[:, parity, cols], job.ps).then_inc(job.free, 1)

            def put_shift_factor(job, n, parity):
                act.wait_ge(job.free, job.turn + 1)
                cols = slice(n * HALF, (n + 1) * HALF)
                act.activation(k_shift[:, parity, cols], k_hi_lo[:, parity, cols], ACT.Identity,
                               scale=shift_mul[:, 0:1], bias=shift_add[:, 0:1]).then_inc(k_shift_ready, 1)

            def copy_head(head):
                if isinstance(head, int):
                    act.copy(h_head[:, :], hT[:, head * P:(head + 1) * P]).then_inc(head_copied, 1)
                else:
                    act.copy(h_head[:, :], hT[:, bass.ds(head * P, P)]).then_inc(head_copied, 1)

            def copy_pv(unit_done):
                act.wait_ge(pv_done, PAIRS * unit_done)
                act.copy(oT[:, :], ps[:, PV_BANK:PV_BANK + 2, :].rearrange("p a b -> p (a b)")).then_inc(o_copied, 1)

            act.wait_ge(kept_dve, 5)
            act.wait_ge(kept_act, 5)
            copy_head(0)
            for local, (kind, i) in enumerate(PROLOGUE):
                side(Job(None, local), kind, i, 0)
                if kind == "k" and i % 2:
                    act.wait_ge(consts, 6)
                    put_shift_factor(Job(None, local), i // 2, 0)

            def body(t, _):
                local = 0
                k_jobs = {}
                for p, half, head, unit, plan in units(t):
                    first = isinstance(t, int) and t == 0 and p == 0 and half == 0
                    last_head = isinstance(t, int) and t == END_T and p == 1
                    if half == 0 and not last_head:
                        copy_head(head + 1)
                    for step, places in enumerate(plan):
                        for place, jobs in enumerate(places):
                            if place < 2:
                                kt = 2 * step + place
                                act.wait_ge(scored, unit * TILES + (kt + 1))
                                if not (first and kt < PROBS):
                                    old = kt - PROBS
                                    if kt % 2 == 0:
                                        act.wait_ge(pv_done, unit * PAIRS + (old // 2 + 1))
                                    act.wait_ge(added, unit * (TILES - 1) + (adds(old % TILES)
                                                - (TILES - 1 if old < 0 else 0)))
                                act.activation(probs[:, kt % PROBS, :],
                                               ps[:, 2 * place:2 * place + 2, :].rearrange("p a b -> p (a b)"),
                                               ACT.Exp, scale=SCALE).then_inc(exped, 1)
                            for kind, i in jobs:
                                if kind == "k":
                                    k_jobs[i] = Job(t, local)
                                side(Job(t, local), kind, i, 1 - p)
                                local += 1
                            if step == PAIRS - 1 and place < 2 and half == 0 and not last_head:
                                put_shift_factor(k_jobs[2 * place + 1], place, 1 - p)
                        if step == 0 and not first:
                            copy_pv(unit)
                        if step == 1 and last_head and half == 1:
                            layernorm_root(act, range(READY_BLOCKS), 2)

            pairs_of_heads(act, body)
            copy_pv(UNITS)
            for k, (kind, i) in enumerate(EPILOGUE):
                side(Job(END_T, LAST_LOCAL + k), kind, i, None)
            keep_spread(act, 0)
            keep_spread(act, 1)
            ffn_act(act)

        @block.gpsimd
        def _(pool):
            pool.memset(ident[:, :], 0.0).then_inc(consts, 1)
            pool.memset(ones[:, :], 1.0).then_inc(consts, 1)
            pool.wait_ge(consts, 2)
            pool.affine_select(out=ident[:, :], in_=ident[:, :], compare_op=ALU.not_equal, fill=1.0, base=0,
                               pattern=[[-1, P]], channel_multiplier=1).then_inc(consts, 1)
            pool.memset(eps[:, :], EPS).then_inc(consts, 1)
            pool.wait_ge(consts, 3)
            row = ident[:, SHIFT_ROW:SHIFT_ROW + 1]
            pool.tensor_scalar(shift_mul[:, :], row, -1.0, 1.0, ALU.mult, ALU.add).then_inc(consts, 1)
            pool.tensor_scalar(shift_add[:, :], row, -1.0, None, ALU.mult).then_inc(consts, 1)
            pool.memset(earlier[:, :, :], 0.0).then_inc(consts, 1)
            pool.wait_ge(consts, 7)
            for e in range(1, EXPERTS):
                pool.memset(earlier[:, e, 0:e], 1.0).then_inc(consts, 1)
            pool.memset(weight_nat[:, :, :], 0.0).then_inc(consts, 1)

            def add_tile(unit, half, kt):
                pool.wait_ge(exped, unit * TILES + (kt + 1))
                total = acc[:, half, :]
                if kt > 1:
                    pool.wait_ge(added, unit * (TILES - 1) + (kt - 1))
                pool.tensor_tensor(total, total if kt > 1 else probs[:, 0, :], probs[:, kt % PROBS, :],
                                   ALU.add).then_inc(added, 1)

            def sum_head(job, head):
                pool.wait_ge(job.free, job.turn + 1)
                for k, n in enumerate((8, 4, 2, 1)):
                    pool.tensor_tensor(y_parts[:, 0:n, :], y_parts[:, 0:n, :], y_parts[:, n:2 * n, :],
                                       ALU.add).then_inc(tree, 1)
                    pool.wait_ge(tree, head * 4 + (k + 1))
                at = slice(head, head + 1) if isinstance(head, int) else bass.ds(head, 1)
                pool.tensor_tensor(x_mid[:, at, :], y_parts[:, 0:1, :], x_in[:, at, :], ALU.add).then_inc(mid_ready, 1)

            def body(t, _):
                local = 0
                for p, half, head, unit, plan in units(t):
                    first = isinstance(t, int) and t == 0 and p == 0 and half == 0
                    for step, places in enumerate(plan):
                        for place, jobs in enumerate(places):
                            kt = 2 * step + place
                            if 0 < kt < 2 * step + 2:
                                add_tile(unit, half, kt)
                            for kind, i in jobs:
                                if kind == "out" and i == 1 and half == 0 and not first:
                                    sum_head(Job(t, local), head - 1)
                                local += 1

            pairs_of_heads(pool, body)
            weigh_tokens(pool, 0)
            weigh_tokens(pool, 1)
            sum_head(Job(END_T, LAST_LOCAL + EPILOGUE.index(("out", 1))), HEADS - 1)
            for m in range(2, ITEMS):
                weigh_tokens(pool, m)

        @block.vector
        def _(dve):
            links = [0]

            def link(ins):
                links[0] += 1
                ins.then_inc(dve_chain, 1)
                dve.wait_ge(dve_chain, links[0])

            dve.wait_ge(cond_exp, 1)
            link(dve.tensor_scalar(cond_c[:, 2:3], cond_c[:, 1:2], 1.0, None, ALU.add))
            link(dve.reciprocal(cond_c[:, 3:4], cond_c[:, 2:3]))
            dve.tensor_tensor(cond_c[:, 1:2], cond_c[:, 0:1], cond_c[:, 3:4], ALU.mult).then_inc(mod_psum, 1)
            dve.wait_ge(x_loaded, 32)
            layernorm_stats(dve, link, x_in, range(BLOCKS))
            layernorm_apply(dve, link, x_in, x_mid, range(BLOCKS), 1)
            dve.wait_ge(mod_psum, 2)
            link(dve.tensor_copy(mod[:, :], ps[:, 7, 0:6]))
            gates = mod[:, 2:6:3]
            link(dve.tensor_scalar(mod_t[:, 0, :], gates, 0.0, None, ALU.is_ge))
            link(dve.tensor_scalar(mod_t[:, 1, :], mod_t[:, 0, :], 2.0, -1.0, ALU.mult, ALU.add))
            link(dve.tensor_tensor(mod_t[:, 2, :], mod_t[:, 1, :], gates, ALU.mult))
            link(dve.tensor_scalar(mod_t[:, 3, :], mod_t[:, 2, :], 0.25, None, ALU.max))
            link(dve.tensor_tensor(gates, mod_t[:, 3, :], mod_t[:, 1, :], ALU.mult))
            link(dve.tensor_scalar(mod[:, 1:5:3], mod[:, 1:5:3], 1.0, None, ALU.add))
            dve.wait_ge(w_loaded["wo"], 32)
            dve.tensor_scalar(wo_nat, wo_nat, mod[:, 2:3], None, ALU.mult).then_inc(mod_ready, 1)
            dve.wait_ge(w_loaded["ffn"], 96)
            dve.tensor_scalar(w2_nat, w2_nat, mod[:, 5:6], None, ALU.mult).then_inc(folded, 1)
            dve.tensor_scalar(sw2_nat, sw2_nat, mod[:, 5:6], None, ALU.mult).then_inc(folded, 1)
            for n, (name, i) in enumerate(SETUP):
                if n % 2:
                    continue
                dve.wait_ge(turned, n + 1)
                src = ps[:, n % 8, :]
                if name == "h":
                    dve.tensor_scalar(hT[:, i * BANK:(i + 1) * BANK], src, mod[:, 1:2], mod[:, 0:1],
                                      ALU.mult, ALU.add).then_inc(kept_dve, 1)
                else:
                    for dst, s in setup_copies(name, i, src)[:-1]:
                        dve.tensor_copy(dst, s)
                    dst, s = setup_copies(name, i, src)[-1]
                    dve.tensor_copy(dst, s).then_inc(kept_dve, 1)

            def side(job, kind, i, target_unit, target_half, high, parity, head_before, last_half):
                if kind in ("v", "turn", "logits", "weights"):
                    return
                dve.wait_ge(side_full, job.full)
                cols = slice(i * BANK, (i + 1) * BANK)
                if kind == "q":
                    dve.wait_ge(hi_ready, high)
                    dve.tensor_tensor(q_lo[:, parity, cols], job.ps, q_hi[:, parity, cols],
                                      ALU.subtract).then_inc(job.free, 1)
                if kind == "k":
                    dve.wait_ge(hi_ready, high)
                    low = k_hi_lo[HEAD_DIM:P, parity, cols]
                    dve.tensor_tensor(low, job.ps[HEAD_DIM:P, :], low, ALU.subtract).then_inc(job.free, 1)
                if kind == "peak":
                    dve.tensor_reduce(peak_parts[:, i:i + 1], job.ps, AX.X, ALU.max).then_inc(job.free, 1)
                    if i == PEAKS - 1:
                        dve.wait_ge(job.free, job.turn + 1)
                        dve.wait_ge(side_free[1 - job.bank], job.turn + job.bank)
                        dve.tensor_reduce(peak[:, :], peak_parts[:, :].rearrange("p (c b) -> p c b", b=4),
                                          AX.X, ALU.max).then_inc(peak_ready, 1)
                if kind == "shift":
                    if not (isinstance(target_unit, int) and target_unit < 2):
                        dve.wait_ge(shift_ready, target_unit * 16 - 16)
                    dve.tensor_copy(shift_sb[:, target_half, :], job.ps[0:8, 0:P]).then_inc(job.free, 1)
                if kind == "sum":
                    dve.reciprocal(inv_sum[:, last_half, :], job.ps[:, 0:8]).then_inc(job.free, 1)
                    dve.wait_ge(job.free, job.turn + 1)
                if kind == "out":
                    if i == 0 and last_half == 0 and not (isinstance(head_before, int) and head_before == 0):
                        dve.wait_ge(mid_ready, head_before)
                    chunk = 8 * last_half + 4 * i
                    dve.tensor_tensor(y_parts[:, chunk:chunk + 4, :], job.ps.rearrange("p (c d) -> p c d", d=DIM),
                                      inv_sum[:, last_half, 4 * i:4 * i + 4, None].broadcast_to([P, 4, DIM]),
                                      ALU.mult).then_inc(job.free, 1)

            for local, (kind, i) in enumerate(PROLOGUE):
                high = PROJECTIONS.index((kind, i)) + 1 if kind in "qk" else 0
                side(Job(None, local), kind, i, 0, 0, high, 0, None, None)

            def body(t, _):
                local = 0
                for p, half, head, unit, plan in units(t):
                    last_unit = isinstance(t, int) and t == END_T and p == 1 and half == 1
                    if last_unit:
                        dve.wait_ge(mid_ready, READY_BLOCKS)
                        layernorm_stats(dve, link, x_mid, range(READY_BLOCKS))
                        layernorm_apply(dve, link, x_mid, x_in, range(READY_BLOCKS), 2)
                        make_select(dve)
                    for places in plan:
                        for jobs in places:
                            for kind, i in jobs:
                                high = head * 8 + (8 + PROJECTIONS.index((kind, i)) + 1 if kind in "qk" else 0)
                                side(Job(t, local), kind, i, unit + 1, 1 - half, high, 1 - p, head - 1 + half,
                                     1 - half)
                                if kind == "logits":
                                    dve.wait_ge(consts, 8 + EXPERTS - 1)
                                    gate(dve, link, Job(t, local), 0)
                                local += 1

            pairs_of_heads(dve, body)
            for k, (kind, i) in enumerate(EPILOGUE):
                job = Job(END_T, LAST_LOCAL + k)
                side(job, kind, i, None, None, None, None, HEADS - 1, 1)
            ffn_dve(dve, link)

        @block.tensor
        def _(pe):
            pe.wait_ge(mod_psum, 1)
            pe.wait_ge(wmod_loaded, 16)
            for i in range(6):
                mm = pe.matmul(ps[:, 7, i:i + 1], wmod_nat[:, i * P:(i + 1) * P], cond_c[:, 1:2], start=True, stop=True)
            mm.then_inc(mod_psum, 1)
            pe.wait_ge(consts, 3)
            for n, (name, i) in enumerate(SETUP):
                if n == 7:
                    pe.wait_ge(mod_ready, 1)
                if n >= 8:
                    pe.wait_ge(kept_act if n % 2 else kept_dve, (n - 8) // 2 + 1)
                bank = ps[:, n % 8, :]
                if name in ("wq", "wk", "wv"):
                    pe.wait_ge(w_loaded[name], 16)
                    nat = {"wq": wq_nat, "wk": wk_nat, "wv": wv_nat}[name]
                    for k in range(4):
                        mm = pe.transpose(bank[:, k * P:(k + 1) * P], nat[:, (4 * i + k) * P:(4 * i + k + 1) * P],
                                          ident[:, :])
                if name == "h":
                    for k in range(4):
                        pe.wait_ge(normed, 4 * i + k + 1)
                        mm = pe.transpose(bank[:, k * P:(k + 1) * P], x_mid[:, 4 * i + k, :], ident[:, :])
                if name == "wo":
                    pe.wait_ge(mod_ready, 1)
                    for k in range(4):
                        mm = pe.transpose(bank[:, k * P:(k + 1) * P], wo_nat[:, 4 * i + k, :], ident[:, :])
                if name in ("w1", "w2", "w3"):
                    if name == "w1" and i == 0:
                        pe.wait_ge(w_loaded["ffn"], 96)
                        pe.wait_ge(folded, 2)
                    nat, shared = {"w1": (w1_nat, sw1_nat), "w2": (w2_nat, sw2_nat), "w3": (w3_nat, sw3_nat)}[name]
                    for k in range(3):
                        e = 3 * i + k
                        mm = pe.transpose(bank[:, k * P:(k + 1) * P], nat[:, e, :] if e < EXPERTS else shared,
                                          ident[:, :])
                if name == "gate":
                    pe.wait_ge(w_loaded["small"], 32)
                    pe.transpose(bank[:, 0:EXPERTS], gate_nat[:, :], ident[0:EXPERTS, 0:EXPERTS])
                    mm = pe.matmul(bank[:, EXPERTS:2 * EXPERTS], ones[0:1, :], bias_row[:, :], start=True, stop=True)
                mm.then_inc(turned, 1)

            def side(job, kind, i, parity, target_parity, target_half, target_unit, heads_copied,
                     before_unit, last_half):
                if job.has_earlier:
                    pe.wait_ge(job.free, job.turn)
                bank = job.ps
                if kind in ("q", "k"):
                    if kind == "q" and i == 0:
                        pe.wait_ge(head_copied, heads_copied)
                    w = wq2 if kind == "q" else wk2
                    for k in range(4):
                        mm = pe.matmul(bank[:, k * P:(k + 1) * P], w[:, 4 * i + k, :], h_head[:, :],
                                       start=True, stop=True)
                if kind == "v":
                    mm = pe.matmul(bank, h_head[:, :], wvT[:, i * BANK:(i + 1) * BANK], start=True, stop=True)
                if kind == "peak":
                    q = target_half * HALF + (i // 4) * P
                    mm = pe.matmul(bank, q_hi[:, target_parity, q:q + P],
                                   k_hi_lo[:, target_parity, (i % 4) * BANK:(i % 4 + 1) * BANK], start=True, stop=True)
                if kind == "shift":
                    pe.wait_ge(peak_ready, target_unit + 1)
                    mm = pe.transpose(bank[0:8, 0:P], peak[:, :], ident[:, :])
                if kind == "sum":
                    pe.wait_ge(added, before_unit * (TILES - 1) + (TILES - 1))
                    for c in range(8):
                        mm = pe.matmul(bank[:, c:c + 1], acc[:, last_half, c * P:(c + 1) * P], ones[:, 0:1],
                                       start=True, stop=True)
                if kind == "out":
                    if i == 0:
                        pe.wait_ge(o_copied, before_unit + 1)
                    for k in range(4):
                        c = 4 * i + k
                        mm = pe.matmul(bank[:, k * P:(k + 1) * P], oT[:, c * P:(c + 1) * P],
                                       wo2[:, 8 * last_half + c, :], start=True, stop=True)
                if kind == "turn":
                    for k in range(4):
                        pe.wait_ge(normed, BLOCKS + 4 * i + k + 1)
                        mm = pe.transpose(bank[:, k * P:(k + 1) * P], x_in[:, 4 * i + k, :], ident[:, :])
                if kind == "logits":
                    pe.wait_ge(side_free[1 - job.bank], job.full - 1 - job.turn)
                    for k, b in enumerate(gating_blocks(i)):
                        mm = pe.matmul(bank[:, k * EXPERTS:(k + 1) * EXPERTS], hT[:, b * P:(b + 1) * P], gateT[:, :],
                                       start=True, stop=True)
                if kind == "weights":
                    pe.wait_ge(weights_ready, 1 if i < 3 else 2)
                    for k in range(4):
                        mm = pe.transpose(bank[0:LOW_ROW + EXPERTS, k * P:(k + 1) * P], weight_nat[:, 4 * i + k, :],
                                          ident[:, :])
                mm.then_inc(side_full, 1)

            def scores(p, half, head, unit, kt):
                slot = 2 * (kt % 2)
                q = half * HALF
                first = isinstance(unit, int) and unit == 0
                if not (first and kt < 2):
                    pe.wait_ge(exped, unit * TILES + (kt - 1))
                for b in range(2):
                    pe.matmul(ps[:, slot + b, :], k_hi_lo[:, p, kt * P:(kt + 1) * P],
                              q_hi[:, p, q + b * BANK:q + (b + 1) * BANK], start=True, stop=False)
                if kt == 0:
                    if half == 0:
                        pe.wait_ge(k_shift_ready, head * 2 + 2)
                    pe.wait_ge(shift_ready, unit * 16 + 16)
                for b in range(2):
                    mm = pe.matmul(ps[:, slot + b, :], k_shift[:, p, kt * P:(kt + 1) * P],
                                   q_lo[:, p, q + b * BANK:q + (b + 1) * BANK], start=False, stop=True)
                mm.then_inc(scored, 1)

            def weigh(p, unit, pair, b):
                if b == 0:
                    if not (isinstance(unit, int) and unit == 0) and pair == 0:
                        pe.wait_ge(o_copied, unit)
                    pe.wait_ge(exped, unit * TILES + (2 * pair + 2))
                for k in range(2):
                    kt = 2 * pair + k
                    at = HEAD_DIM * k
                    mm = pe.matmul(ps[at:at + HEAD_DIM, PV_BANK + b, :], v_sb[:, p, kt * HEAD_DIM:(kt + 1) * HEAD_DIM],
                                   probs[:, kt % PROBS, b * BANK:(b + 1) * BANK],
                                   start=(pair == 0), stop=(pair == PAIRS - 1), tile_position=(0, at))
                if b == 1:
                    mm.then_inc(pv_done, 1)

            pe.wait_ge(kept_act, len(SETUP) // 2)
            pe.wait_ge(kept_dve, (len(SETUP) + 1) // 2)
            for local, (kind, i) in enumerate(PROLOGUE):
                side(Job(None, local), kind, i, 0, 0, 0, 0, 1, None, None)

            def body(t, _):
                local = 0
                for p, half, head, unit, plan in units(t):
                    first = isinstance(t, int) and t == 0 and p == 0 and half == 0
                    for step, places in enumerate(plan):
                        for place, jobs in enumerate(places):
                            if place < 2:
                                scores(p, half, head, unit, 2 * step + place)
                            elif step > 0:
                                weigh(p, unit, step - 1, place - 2)
                            elif not first:
                                weigh(p if half else 1 - p, unit - 1, PAIRS - 1, place - 2)
                            for kind, i in jobs:
                                side(Job(t, local), kind, i, 1 - p, p if half == 0 else 1 - p, 1 - half, unit + 1,
                                     head + 2, unit - 1, 1 - half)
                                local += 1

            pairs_of_heads(pe, body)
            for b in range(2):
                weigh(1, UNITS - 1, PAIRS - 1, b)
            for k, (kind, i) in enumerate(EPILOGUE):
                if kind == "sum":
                    spread(pe, 0)
                    spread(pe, 1)
                side(Job(END_T, LAST_LOCAL + k), kind, i, None, None, None, None, None, UNITS - 1, 1)
            ffn_pe(pe, side)


_INS = ['L0_attn_x', 'L0_attn_wq', 'L0_attn_wk', 'L0_attn_wv', 'L0_attn_wo', 'L0_ffn_gate_w', 'L0_ffn_w1',
        'L0_ffn_w2', 'L0_ffn_w3', 'L0_ffn_sw1', 'L0_ffn_sw2', 'L0_ffn_sw3', 'L0_ffn_expert_bias', 'L0_c', 'L0_wmod']
_OUTS = [((1, TOKENS, DIM), 'float32')]


def kernel(**inputs):
    import numpy as _np
    import concourse.bacc as _bacc
    from concourse import mybir as _mybir
    from concourse.bass_utils import run_bass_kernel_spmd as _run

    nc = _bacc.Bacc("TRN2", target_bir_lowering=False, num_devices=1)
    arrays, args = {}, []
    for name in _INS:
        a = _np.ascontiguousarray(inputs[name])
        arrays[f"in_{name}_dram"] = a
        args.append(nc.dram_tensor(f"in_{name}_dram", a.shape, _mybir.dt.from_np(a.dtype), kind="ExternalInput").ap())
    for i, (shape, dtype) in enumerate(_OUTS):
        dt = _mybir.dt.from_np(_np.dtype(dtype))
        args.append(nc.dram_tensor(f"out_{i}_dram", shape, dt, kind="ExternalOutput").ap())
    build(nc, *args)
    r = _run(nc, [arrays], core_ids=[0])
    got = tuple(r.results[0][f"out_{i}_dram"] for i in range(len(_OUTS)))
    return got[0]
```

```python
from contextlib import ExitStack

import concourse.bass as bass
from concourse import mybir

F32 = mybir.dt.float32
F32R = mybir.dt.float32r
ALU = mybir.AluOpType
ACT = mybir.ActivationFunctionType
AX = mybir.AxisListType

P = 128
TOKENS, DIM = 2048, 128
HEADS, HEAD_DIM = 16, 64
BLOCKS = TOKENS // P
CHUNKS = HEADS
POSITIONS = P * CHUNKS
HALF = POSITIONS // 2
BANK = 512
TILES = CHUNKS
PAIRS = TILES // 2
UNITS = 2 * HEADS
EXPERTS, HID = 8, 128
SCALE = HEAD_DIM ** -0.5
EPS = 1e-5
SHIFT_ROW = 64
STAGES = 3
PROBS = 8

PV_BANK, SIDE_BANK = 4, 6

PEAKS = 32


LONG_JOBS = (
    {2: ("q", 0), 6: ("k", 0), 10: ("k", 1), 13: ("sum", 0), 17: ("out", 0), 21: ("out", 1)},
    {2: ("q", 1), 6: ("v", 0), 10: ("v", 1), 13: ("sum", 0), 17: ("out", 0), 21: ("out", 1)},
)
PEAK_PLACES = 26
LAST_UNIT_JOBS = {8: ("turn", 0), 9: ("turn", 1), 10: ("turn", 2), 11: ("logits", 0)}
READY_BLOCKS = 12
PROJECTIONS = [("q", 0), ("k", 0), ("k", 1), ("q", 1), ("v", 0), ("v", 1)]


def chunk_of(slot):
    return slot // 8 * 8 + slot % 4 * 2 + slot % 8 // 4


def side_jobs(half, last_unit_jobs=True, project=True, peaks=True, last_unit=False):
    places = [[] for _ in range(4 * PAIRS)]
    for place, job in LONG_JOBS[half].items():
        if last_unit_jobs if job[0] in ("sum", "out") else project:
            places[place].append(job)
    if peaks:
        peak = 0
        for place in range(PEAK_PLACES):
            single = lambda p: p in LONG_JOBS[half] or (p - 1) in LONG_JOBS[half]
            singles, done = sum(map(single, range(PEAK_PLACES))), sum(map(single, range(place + 1)))
            upto = done + -(-(PEAKS - singles) * (place + 1 - done) // (PEAK_PLACES - singles))
            places[place][:0] = [("peak", i) for i in range(peak, upto)]
            peak = upto
        places[4 * (PAIRS - 1)].append(("shift", 0))
    if last_unit:
        for place, job in LAST_UNIT_JOBS.items():
            places[place].append(job)
    return [places[4 * step:4 * step + 4] for step in range(PAIRS)]


def build(nc, x, wq, wk, wv, wo, gate_w, w1, w2, w3, sw1, sw2, sw3, expert_bias, cond, wmod, out):
    with ExitStack() as ctx:
        def sb(name, shape, dt=F32):
            return ctx.enter_context(nc.sbuf_tensor(name, shape, dt))

        def sem(name):
            return ctx.enter_context(nc.semaphore(name))

        x_in = sb("x_in", [P, BLOCKS, DIM])
        x_mid = sb("x_mid", [P, BLOCKS, DIM])
        hT = sb("hT", [P, TOKENS])
        h_head = sb("h_head", [P, P])
        wqT = sb("wqT", [P, CHUNKS * HEAD_DIM])
        wkT = sb("wkT", [P, CHUNKS * HEAD_DIM])
        stage_hi = sb("stage_hi", [P, STAGES, BANK], F32R)
        stage_lo = sb("stage_lo", [P, STAGES, BANK], F32R)
        token_weights = sb("token_weights", [P, 4, BANK])
        wvT = sb("wvT", [P, CHUNKS * HEAD_DIM])
        wo2 = sb("wo2", [P, CHUNKS, DIM])
        q_hi = sb("q_hi", [P, 2, POSITIONS], F32R)
        q_lo = sb("q_lo", [P, 2, POSITIONS], F32R)
        k_hi_lo = sb("k_hi_lo", [P, 2, POSITIONS], F32R)
        k_shift = sb("k_shift", [P, 2, POSITIONS], F32R)
        v_sb = sb("v_sb", [P, 2, CHUNKS * HEAD_DIM])
        probs = sb("probs", [P, PROBS, HALF])
        acc = sb("acc", [P, 2, HALF])
        oT = sb("oT", [P, HALF])
        w1T = sb("w1T", [P, EXPERTS + 1, HID])
        w3T = sb("w3T", [P, EXPERTS + 1, HID])
        w2T = sb("w2T", [P, EXPERTS + 1, DIM])
        ident = sb("ident", [P, P])
        ones = sb("ones", [P, P])
        eps = sb("eps", [P, 1])
        stats = sb("stats", [P, BLOCKS, 6])
        mean_var = sb("mean_var", [P, BLOCKS, 2])
        std = sb("std", [P, BLOCKS])
        rstd = sb("rstd", [P, BLOCKS])
        shift_ln = sb("shift_ln", [P, BLOCKS])
        cond_c = sb("cond_c", [P, 4])
        mod = sb("mod", [P, 6])
        mod_t = sb("mod_t", [P, 4, 2])
        peak_parts = sb("peak_parts", [P, PEAKS])
        peak = sb("peak", [P, 8])
        shift_sb = sb("shift_sb", [8, 2, P], F32R)
        inv_sum = sb("inv_sum", [P, 2, 8])
        y_parts = sb("y_parts", [P, CHUNKS, DIM])
        gateT = sb("gateT", [P, EXPERTS])
        gate_nat = sb("gate_nat", [EXPERTS, DIM])
        bias_row = sb("bias_row", [1, EXPERTS])
        bias_sb = sb("bias_sb", [P, EXPERTS])
        earlier = sb("earlier", [P, EXPERTS, EXPERTS])
        ps = ctx.enter_context(nc.psum_tensor("ps", [P, 8, BANK], F32))

        wq_nat, wk_nat, wv_nat, wmod_nat = (probs[:, i, :] for i in range(4))
        wo_nat = probs[:, 4:6, :].rearrange("p a (c d) -> p (a c) d", d=P)
        w1_nat, w3_nat = (probs[:, 6 + i, :].rearrange("p (e d) -> p e d", d=P) for i in range(2))
        w2_nat = oT[:, :].rearrange("p (e d) -> p e d", d=P)
        sw1_nat, sw3_nat, sw2_nat = (acc[:, 0, i * P:(i + 1) * P] for i in range(3))

        first_loaded = sem("first_loaded")
        x_loaded, cond_loaded, wmod_loaded = sem("x_loaded"), sem("cond_loaded"), sem("wmod_loaded")
        w_loaded = {n: sem(n + "_loaded") for n in ("wq", "wk", "wv", "wo", "ffn", "small")}
        consts, minus_one = sem("consts"), sem("minus_one")
        cond_exp, mod_ready, mod_psum = sem("cond_exp"), sem("mod_ready"), sem("mod_psum")
        ln_step, std_ready = sem("ln_step"), sem("std_ready")
        normed, normed_pool = sem("normed"), sem("normed_pool")
        folded = sem("folded")
        first_turned = sem("first_turned")
        turned = sem("turned")
        kept = sem("kept")
        warm, shift_ln_ready = sem("warm"), sem("shift_ln_ready")
        dve_chain = sem("dve_chain")
        head_copied = sem("head_copied")
        side_full = sem("side_full")
        side_free = [sem("side_free0"), sem("side_free1")]
        hi_ready = sem("hi_ready")
        placed = [sem("placed0"), sem("placed1"), sem("placed2")]
        placed_low = [sem("placed_low0"), sem("placed_low1"), sem("placed_low2")]
        peak_ready = sem("peak_ready")
        shift_ready = sem("shift_ready")
        scored, exped, pv_done, o_copied = sem("scored"), sem("exped"), sem("pv_done"), sem("o_copied")
        added = sem("added")
        tree, mid_ready = sem("tree"), sem("mid_ready")
        stored = [sem("stored0"), sem("stored1")]

        block = ctx.enter_context(nc.Block())

        FULL_JOBS = sum(len(p) for f in (0, 1) for s in side_jobs(f) for p in s)
        PROLOGUE_JOBS = len(PROJECTIONS) + PEAKS + 1
        FIRST_MISSING = 3
        STEADY_BASE = PROLOGUE_JOBS - FIRST_MISSING

        def job_number(t, local):
            if isinstance(t, int) and t == 0:
                return PROLOGUE_JOBS + local
            return t * (2 * FULL_JOBS) + (STEADY_BASE + local)

        def bank_of(t, local):
            return (PROLOGUE_JOBS + local) % 2 if isinstance(t, int) and t == 0 else (STEADY_BASE + local) % 2

        def bank_turn(t, local):
            if isinstance(t, int) and t == 0:
                return (PROLOGUE_JOBS + local) // 2
            return t * FULL_JOBS + (STEADY_BASE + local) // 2

        class Job:

            def __init__(self, t, local):
                self.bank = bank_of(t, local) if t is not None else local % 2
                self.turn = bank_turn(t, local) if t is not None else local // 2
                self.full = (job_number(t, local) if t is not None else local) + 1
                self.has_earlier = t is not None or local >= 2
                self.ps = ps[:, SIDE_BANK + self.bank, :]
                self.may_use = self.turn
                if t is None:
                    if local % 4 >= 2:
                        self.ps = ps[:, PV_BANK + self.bank, :]
                    if local < PROLOGUE.index(("shift", 0)):
                        self.has_earlier = local >= 4
                        self.may_use = self.turn - 1
                self.free = side_free[self.bank]

        def adds(kt):
            return max(1, kt)

        def pairs_of_heads(eng, body):
            body(0)
            with eng.Fori(1, HEADS // 2 - 1) as t:
                body(t)
            body(HEADS // 2 - 1)

        def units(t):
            first, last = (isinstance(t, int) and t == 0), (isinstance(t, int) and t == HEADS // 2 - 1)
            for p in (0, 1):
                for half in (0, 1):
                    final_head = last and p == 1
                    plan = side_jobs(half, last_unit_jobs=not (first and p == 0 and half == 0),
                                     project=not final_head, peaks=not (final_head and half == 1),
                                     last_unit=final_head and half == 1)
                    yield p, half, t * 2 + p, t * 4 + (2 * p + half), plan

        PROLOGUE = PROJECTIONS[:3] + [("peak", i) for i in range(16)] + PROJECTIONS[3:4] \
            + [("peak", i) for i in range(16, PEAKS)] + [("shift", 0)] + PROJECTIONS[4:]
        SENDS = 64

        def stage_of(kind, i):
            return PROJECTIONS.index((kind, i)) % STAGES

        def sends(kind, i, head, before=False):
            n = PROJECTIONS.index((kind, i))
            uses = 2 if n % STAGES == 0 else 1
            return head * (uses * SENDS) + (n // STAGES + (0 if before else 1)) * SENDS

        EPILOGUE = [("weights", 0), ("weights", 1), ("weights", 2), ("sum", 0), ("out", 0), ("out", 1)]
        END_T = HEADS // 2 - 1
        LAST_LOCAL = sum(len(pl) for _, _, _, _, plan in units(END_T) for s in plan for pl in s)

        ALL_JOBS = job_number(END_T, LAST_LOCAL + len(EPILOGUE))

        class LateJob:

            def __init__(self, n):
                self.bank, self.turn, self.full = 1, ALL_JOBS // 2 + n, ALL_JOBS + n + 1
                self.has_earlier, self.may_use = True, self.turn
                self.ps = ps[:, SIDE_BANK + 1, :]
                self.free = side_free[1]

        LATE = [("turn", 3), ("logits", 1), ("weights", 3)]

        def gating_blocks(i):
            return range(READY_BLOCKS) if i == 0 else range(READY_BLOCKS, BLOCKS)

        FIRST_SETUP = [("wq", 0), ("wq", 1), ("wk", 0), ("wk", 1)]
        SECOND_SETUP = [("wv", 0), ("wv", 1)]
        LATER_SETUP = [("h", i) for i in range(4)] + [("wo", i) for i in range(4)] \
            + [(n, i) for n in ("w1", "w3", "w2") for i in range(3)] + [("gate", 0)]
        SETUP = FIRST_SETUP + SECOND_SETUP + LATER_SETUP
        SETUP_BANKS = 4
        POOL_FROM = 10
        setup_after = {}
        for n in range(len(LATER_SETUP)):
            setup_after.setdefault(5 + n * 26 // len(LATER_SETUP), []).append(len(SETUP) - len(LATER_SETUP) + n)

        def setup_copies(name, i, src):
            by = lambda s, d: s.rearrange("p (c d) -> p c d", d=d)
            if name in ("wq", "wk", "wv"):
                w = {"wq": wqT, "wk": wkT, "wv": wvT}[name]
                return [(w[:, i * BANK:(i + 1) * BANK], src)]
            if name == "wo":
                return [(wo2[:, 4 * i:4 * i + 4, :], by(src, DIM))]
            if name == "h":
                first = P if i == 0 else 0
                return [(hT[:, i * BANK + first:(i + 1) * BANK], src[:, first:])]
            if name == "gate":
                return [(gateT[:, :], src[:, 0:EXPERTS]), (bias_sb[:, :], src[:, EXPERTS:2 * EXPERTS])]
            w = {"w1": w1T, "w3": w3T, "w2": w2T}[name]
            return [(w[:, 3 * i:3 * i + 3, :], by(src[:, 0:3 * P], P))]

        def layernorm_stats(dve, link, src, blocks):
            for b in blocks:
                ins = dve.bn_stats(stats[:, b, :], src[:, b, :])
            link(ins)
            for b in blocks:
                ins = dve.bn_aggr(mean_var[:, b, :], stats[:, b, :])
            ins.then_inc(ln_step, 1)

        def layernorm_rstd(dve, link, blocks, nth):
            dve.wait_ge(std_ready, nth)
            b0, b1 = blocks[0], blocks[-1] + 1
            link(dve.reciprocal(rstd[:, b0:b1], std[:, b0:b1]))

        def layernorm_apply(eng, src, dst, blocks):
            for b in blocks:
                eng.tensor_scalar(dst[:, b, :], src[:, b, :], mean_var[:, b, 0:1], rstd[:, b:b + 1],
                                  ALU.subtract, ALU.mult).then_inc(normed, 1)

        def layernorm_root(act, blocks, nth):
            act.wait_ge(ln_step, nth)
            b0, b1 = blocks[0], blocks[-1] + 1
            act.activation(std[:, b0:b1], mean_var[:, b0:b1, 1], ACT.Sqrt, bias=eps[:, :]).then_inc(std_ready, 1)

        GROUPS = TOKENS // BANK
        ALL = EXPERTS + 1

        def two(buf):
            return [buf[:, 0:BANK], buf[:, BANK:2 * BANK]]

        weighted = two(probs[:, 0, :])
        silu_sb = two(probs[:, 1, :])
        inner = two(probs[:, 2, :])
        inner_w = two(probs[:, 3, :])
        x_out = two(probs[:, 4, :])
        greater = wqT[:, :].rearrange("p (b e j) -> p b e j", e=EXPERTS, j=EXPERTS)
        equal = wkT[:, :].rearrange("p (b e j) -> p b e j", e=EXPERTS, j=EXPERTS)
        token_weight = [token_weights[:, n, :] for n in range(4)]
        small = wvT[:, :].rearrange("p (n b e) -> p n b e", n=8, e=EXPERTS)
        gate_exp, gate_den, score, biased, rank, chosen = (small[:, n] for n in range(6))
        LOW_ROW = 32
        weight_nat = v_sb[:, 0, 0:BLOCKS * (LOW_ROW + EXPERTS)].rearrange("p (b r) -> p b r", b=BLOCKS)
        weight_hi = sb("weight_hi", [P, BLOCKS, EXPERTS], F32R)
        weightT = q_hi[0:LOW_ROW + EXPERTS, 0, :]
        select = k_hi_lo[0:LOW_ROW + EXPERTS, 0, 0:EXPERTS * P].rearrange("p (e m) -> p e m", m=P)

        weights_ready = sem("weights_ready")
        select_ready = sem("select_ready")
        bcast, bcast_kept = sem("bcast"), sem("bcast_kept")
        weighted_ready = sem("weighted_ready")
        ups, silued, inner_ready, inner_w_ready = sem("ups"), sem("silued"), sem("inner_ready"), sem("inner_w_ready")
        downs, out_ready = sem("downs"), sem("out_ready")

        def banks(m):
            return ps[:, 2 + m % 2, :], ps[:, 4 + m % 2, :]

        def routed(m):
            return m // ALL * EXPERTS + min(m % ALL, EXPERTS)

        ITEMS = GROUPS * ALL

        LATE_STATS, LATE_NORM, LATE_GATE = 2, 3, 6
        LATE_AFTER = {4: 0, 5: 1, 8: 2}

        def spread(pe, m):
            if m % ALL == EXPERTS or m >= ITEMS:
                return
            g, e = m // ALL, m % ALL
            if e == 0:
                job = Job(END_T, LAST_LOCAL + EPILOGUE.index(("weights", g))) if g < 3 else LateJob(2)
                pe.wait_ge(job.free, job.turn + 1)
            if m == 0:
                pe.wait_ge(select_ready, 1)
            n = routed(m)
            if n >= 2:
                pe.wait_ge(bcast_kept, n - 1)
            pe.matmul(ps[:, n % 2, :], select[:, e, :], weightT[:, g * BANK:(g + 1) * BANK],
                      start=True, stop=True).then_inc(bcast, 1)

        def keep_spread(act, m):
            if m % ALL == EXPERTS or m >= ITEMS:
                return
            n = routed(m)
            act.wait_ge(bcast, n + 1)
            if n >= 4:
                old = (n - 4) // EXPERTS * ALL + (n - 4) % EXPERTS
                act.wait_ge(inner_w_ready, old + 1)
            act.copy(token_weight[n % 4], ps[:, n % 2, :]).then_inc(bcast_kept, 1)

        def weigh_tokens(pool, m):
            g, e = m // ALL, m % ALL
            if e == EXPERTS:
                return
            n = routed(m)
            pool.wait_ge(bcast_kept, n + 1)
            if m >= 2:
                pool.wait_ge(ups, m - 1)
            pool.tensor_tensor(weighted[m % 2], hT[:, g * BANK:(g + 1) * BANK], token_weight[n % 4],
                               ALU.mult).then_inc(weighted_ready, 1)

        def ffn_pe(pe, side):
            def down(m):
                g, e = m // ALL, m % ALL
                if m == 0:
                    pe.wait_ge(side_free[0], ALL_JOBS - ALL_JOBS // 2)
                if e == 0 and g >= 2:
                    pe.wait_ge(out_ready, g - 1)
                pe.wait_ge(inner_w_ready, m + 1)
                for k in range(4):
                    mm = pe.matmul(ps[:, 6 + g % 2, k * P:(k + 1) * P], inner_w[m % 2][:, k * P:(k + 1) * P],
                                   w2T[:, e, :], start=(e == 0 and k == 0), stop=(e == ALL - 1 and k == 3),
                                   skip_group_check=True)
                mm.then_inc(downs, 1)

            for m in range(ITEMS):
                g, e = m // ALL, m % ALL
                spread(pe, m + 2)
                rhs = hT[:, g * BANK:(g + 1) * BANK] if e == EXPERTS else weighted[m % 2]
                if e < EXPERTS:
                    pe.wait_ge(weighted_ready, routed(m) + 1)
                if m >= 2:
                    pe.wait_ge(inner_ready, m - 1)
                pe.matmul(banks(m)[0], w1T[:, e, :], rhs, start=True, stop=True)
                pe.matmul(banks(m)[1], w3T[:, e, :], rhs, start=True, stop=True).then_inc(ups, 1)
                if m >= 1:
                    down(m - 1)
                if m in LATE_AFTER:
                    side(LateJob(LATE_AFTER[m]), *LATE[LATE_AFTER[m]], None, None, None, None, None, None, None)
            down(ITEMS - 1)

        def gating_act(act, job, kind, i):
            act.wait_ge(side_full, job.full)
            cols = slice(i * BANK, (i + 1) * BANK)
            if kind == "turn":
                act.activation(hT[:, cols], job.ps, ACT.Identity, scale=mod[:, 4:5],
                               bias=mod[:, 3:4]).then_inc(job.free, 1)
            if kind == "logits":
                blocks = gating_blocks(i)
                act.activation(gate_exp[:, blocks[0]:blocks[-1] + 1, :],
                               job.ps[:, 0:len(blocks) * EXPERTS].rearrange("p (b e) -> p b e", e=EXPERTS), ACT.Exp,
                               scale=-1.0).then_inc(job.free, 1)
            if kind == "weights":
                act.copy(weightT[:, cols], job.ps[0:LOW_ROW + EXPERTS, :]).then_inc(job.free, 1)

        def ffn_act(act):
            for m in range(ITEMS):
                keep_spread(act, m + 2)
                act.wait_ge(ups, m + 1)
                if m >= 2:
                    act.wait_ge(inner_ready, m - 1)
                act.activation(silu_sb[m % 2], banks(m)[0], ACT.Silu).then_inc(silued, 1)
                if m == LATE_STATS:
                    layernorm_root(act, range(READY_BLOCKS, BLOCKS), 4)
                if m in LATE_AFTER:
                    gating_act(act, LateJob(LATE_AFTER[m]), *LATE[LATE_AFTER[m]])

        def make_select(dve):
            n = LOW_ROW + EXPERTS
            dve.tensor_tensor(select, ident[0:n, 0:EXPERTS, None].broadcast_to([n, EXPERTS, P]),
                              ident[0:n, LOW_ROW:n, None].broadcast_to([n, EXPERTS, P]),
                              ALU.add).then_inc(select_ready, 1)

        def gate(dve, link, job, i):
            dve.wait_ge(job.free, job.turn + 1)
            blocks = gating_blocks(i)
            at, n = slice(blocks[0], blocks[-1] + 1), len(blocks)
            link(dve.tensor_scalar(gate_den[:, at], gate_exp[:, at], 1.0, None, ALU.add))
            link(dve.reciprocal(score[:, at], gate_den[:, at]))
            link(dve.tensor_tensor(biased[:, at], score[:, at], bias_sb[:, None, :].broadcast_to([P, n, EXPERTS]),
                                   ALU.add))
            mine = biased[:, at, :, None].broadcast_to([P, n, EXPERTS, EXPERTS])
            other = biased[:, at, None, :].broadcast_to([P, n, EXPERTS, EXPERTS])
            dve.tensor_tensor(greater[:, at], other, mine, ALU.is_gt)
            link(dve.tensor_tensor(equal[:, at], other, mine, ALU.is_equal))
            link(dve.tensor_tensor(equal[:, at], equal[:, at], earlier[:, None, :, :].broadcast_to(
                [P, n, EXPERTS, EXPERTS]), ALU.mult))
            link(dve.tensor_tensor(greater[:, at], greater[:, at], equal[:, at], ALU.add))
            link(dve.tensor_reduce(rank[:, at], greater[:, at], AX.X, ALU.add))
            link(dve.tensor_scalar(chosen[:, at], rank[:, at], 1.5, None, ALU.is_lt))
            link(dve.tensor_tensor(gate_den[:, at], chosen[:, at], score[:, at], ALU.mult))
            link(dve.tensor_copy(weight_hi[:, at, :], gate_den[:, at]))
            dve.tensor_copy(weight_nat[:, at, 0:EXPERTS], weight_hi[:, at, :])
            dve.tensor_tensor(weight_nat[:, at, LOW_ROW:LOW_ROW + EXPERTS], gate_den[:, at], weight_hi[:, at, :],
                              ALU.subtract).then_inc(weights_ready, 1)

        def ffn_dve(dve, link):
            def add_up(g):
                dve.wait_ge(downs, ALL * (g + 1))
                if g >= 2:
                    dve.wait_ge(stored[g % 2], 16 * (g // 2))
                dve.tensor_tensor(x_out[g % 2].rearrange("p (b d) -> p b d", d=DIM),
                                  ps[:, 6 + g % 2, :].rearrange("p (b d) -> p b d", d=DIM),
                                  x_mid[:, 4 * g:4 * g + 4, :], ALU.add).then_inc(out_ready, 1)

            for m in range(ITEMS):
                g, e = m // ALL, m % ALL
                dve.wait_ge(silued, m + 1)
                if m >= 2:
                    dve.wait_ge(downs, m - 1)
                if e == EXPERTS:
                    dve.tensor_tensor(inner_w[m % 2], silu_sb[m % 2], banks(m)[1], ALU.mult).then_inc(inner_ready, 1)
                    dve.wait_ge(inner_ready, m + 1)
                    dve.engine_nop().then_inc(inner_w_ready, 1)
                else:
                    dve.tensor_tensor(inner[m % 2], silu_sb[m % 2], banks(m)[1], ALU.mult).then_inc(inner_ready, 1)
                    dve.wait_ge(inner_ready, m + 1)
                    dve.tensor_tensor(inner_w[m % 2], inner[m % 2], token_weight[routed(m) % 4],
                                      ALU.mult).then_inc(inner_w_ready, 1)
                if m == LATE_STATS:
                    dve.wait_ge(mid_ready, HEADS)
                    layernorm_stats(dve, link, x_mid, range(READY_BLOCKS, BLOCKS))
                if m == LATE_NORM:
                    layernorm_rstd(dve, link, range(READY_BLOCKS, BLOCKS), 4)
                    layernorm_apply(dve, x_mid, x_in, range(READY_BLOCKS, BLOCKS))
                if m == LATE_GATE:
                    gate(dve, link, LateJob(1), 1)
                if e == 1 and g > 0:
                    add_up(g - 1)
            add_up(GROUPS - 1)

        def ffn_store(sp):
            for g in range(GROUPS):
                sp.wait_ge(out_ready, g + 1)
                sp.dma_start(out[0, g * BANK:(g + 1) * BANK, :].rearrange("(b p) d -> p b d", p=P),
                             x_out[g % 2].rearrange("p (b d) -> p b d", d=DIM)).then_inc(stored[g % 2], 16)
            for n in (0, 1):
                sp.wait_ge(stored[n], 16 * (GROUPS // 2))

        @block.sync
        def _(sp):
            sp.dma_start(x_in[:, 0, :], x[0, 0:P, :]).then_inc(first_loaded, 16)
            sp.dma_start(wmod_nat[:, 0:768], wmod).then_inc(wmod_loaded, 16)
            sp.dma_start(wq_nat.rearrange("p (b d) -> p b d", d=DIM),
                         wq.rearrange("(b p) d -> p b d", p=P)).then_inc(w_loaded["wq"], 16)
            sp.dma_start(wk_nat.rearrange("p (b d) -> p b d", d=DIM),
                         wk.rearrange("(b p) d -> p b d", p=P)).then_inc(w_loaded["wk"], 16)
            sp.dma_start(x_in[:, 1:16, :], x[0, P:2048, :].rearrange("(b p) d -> p b d", p=P)).then_inc(x_loaded, 16)
            sp.dma_start(wv_nat.rearrange("p (b d) -> p b d", d=DIM),
                         wv.rearrange("(b p) d -> p b d", p=P)).then_inc(w_loaded["wv"], 16)
            wo_c = wo.rearrange("h (c d) -> h c d", d=HEAD_DIM)
            sp.dma_start(wo_nat[:, :, 0:HEAD_DIM], wo_c).then_inc(w_loaded["wo"], 16)
            sp.dma_start(wo_nat[:, :, HEAD_DIM:P], wo_c).then_inc(w_loaded["wo"], 16)
            sp.dma_start(gate_nat[:, :], gate_w).then_inc(w_loaded["small"], 16)
            sp.dma_start(bias_row[:, :], expert_bias.rearrange("(a e) -> a e", a=1)).then_inc(w_loaded["small"], 16)

            def send_shift(job, target_parity, target_half):
                sp.wait_ge(job.free, job.turn + 1)
                sp.dma_start(
                    q_lo[SHIFT_ROW:SHIFT_ROW + 1, target_parity,
                         target_half * HALF:(target_half + 1) * HALF].bitcast(F32),
                    shift_sb[:, target_half, :].bitcast(F32),
                ).then_inc(shift_ready, 16)

            def send_projection(job, kind, i, parity, low):
                sp.wait_ge(job.free, job.turn + 1)
                slot = stage_of(kind, i)
                hi, lo = stage_hi[:, slot, :], stage_lo[:, slot, :]
                signal = (placed_low if low else placed)[slot]
                for odd in (0, 1):
                    at, to = odd * HEAD_DIM, slice(i * HALF + odd * BANK, i * HALF + (odd + 1) * BANK)
                    if kind == "q":
                        src, dst = (lo, q_lo) if low else (hi, q_hi)
                        pairs = [(dst[0:HEAD_DIM, parity, to], src[at:at + HEAD_DIM, :]),
                                 (dst[HEAD_DIM:P, parity, to], src[at:at + HEAD_DIM, :])]
                    elif low:
                        pairs = [(k_shift[0:HEAD_DIM, parity, to], hi[at:at + HEAD_DIM, :]),
                                 (k_shift[SHIFT_ROW + 1:P, parity, to], lo[at + 1:at + HEAD_DIM, :])]
                    else:
                        pairs = [(k_hi_lo[0:HEAD_DIM, parity, to], hi[at:at + HEAD_DIM, :]),
                                 (k_hi_lo[HEAD_DIM:P, parity, to], lo[at:at + HEAD_DIM, :])]
                    for dst, src in pairs:
                        sp.dma_start(dst.bitcast(F32), src.bitcast(F32)).then_inc(signal, 16)

            for kind, i, low in (("q", 0, 0), ("k", 0, 0), ("k", 1, 0), ("q", 0, 1), ("k", 0, 1), ("k", 1, 1),
                                 ("q", 1, 0), ("q", 1, 1)):
                if (kind, i, low) == ("q", 0, 1):
                    sp.dma_start(w1_nat, w1.rearrange("e f d -> f e d")).then_inc(w_loaded["ffn"], 16)
                    sp.dma_start(w3_nat, w3.rearrange("e f d -> f e d")).then_inc(w_loaded["ffn"], 16)
                    sp.dma_start(w2_nat, w2.rearrange("e d f -> d e f")).then_inc(w_loaded["ffn"], 16)
                    sp.dma_start(sw1_nat, sw1).then_inc(w_loaded["ffn"], 16)
                    sp.dma_start(sw3_nat, sw3).then_inc(w_loaded["ffn"], 16)
                    sp.dma_start(sw2_nat, sw2).then_inc(w_loaded["ffn"], 16)
                send_projection(Job(None, PROLOGUE.index((kind, i))), kind, i, 0, low)
            send_shift(Job(None, PROLOGUE.index(("shift", 0))), 0, 0)

            def body(t):
                local = 0
                for p, half, head, unit, plan in units(t):
                    for places in plan:
                        for jobs in places:
                            for kind, i in jobs:
                                if kind in ("q", "k"):
                                    for low in (0, 1):
                                        send_projection(Job(t, local), kind, i, 1 - p, low)
                                if kind == "shift":
                                    send_shift(Job(t, local), p if half == 0 else 1 - p, 1 - half)
                                local += 1

            pairs_of_heads(sp, body)
            ffn_store(sp)

        @block.scalar
        def _(act):
            act.dma_start(cond_c[:, 0:1], cond.rearrange("a d -> d a")).then_inc(cond_loaded, 16)
            act.wait_ge(consts, 4)
            act.activation(std[:, 0:1], eps[:, :], ACT.Exp).then_inc(warm, 1)
            act.wait_ge(warm, 1)
            act.wait_ge(cond_loaded, 16)
            act.activation(cond_c[:, 1:2], cond_c[:, 0:1], ACT.Exp, scale=-1.0).then_inc(cond_exp, 1)
            layernorm_root(act, range(1), 1)

            def keep_setup(n):
                name, i = SETUP[n]
                act.wait_ge(turned, n + 1)
                if name == "h" and i == 0:
                    act.wait_ge(mod_ready, 1)
                copies = setup_copies(name, i, ps[:, n % SETUP_BANKS, :])
                for k, (dst, src) in enumerate(copies):
                    if name == "h":
                        ins = act.activation(dst, src, ACT.Identity, scale=mod[:, 1:2], bias=mod[:, 0:1])
                    else:
                        ins = act.copy(dst, src)
                    if k == len(copies) - 1:
                        ins.then_inc(kept, 1)

            for n in range(len(FIRST_SETUP)):
                keep_setup(n)
            def side(job, kind, i, parity, head):
                cols = slice(i * BANK, (i + 1) * BANK)
                if kind in ("turn", "logits", "weights"):
                    gating_act(act, job, kind, i)
                if kind in ("q", "k"):
                    slot = stage_of(kind, i)
                    if not (isinstance(head, int) and sends(kind, i, head, before=True) == 0):
                        act.wait_ge(placed[slot], sends(kind, i, head, before=True))
                        act.wait_ge(placed_low[slot], sends(kind, i, head, before=True))
                    act.wait_ge(side_full, job.full)
                    act.copy(stage_hi[:, slot, :], job.ps).then_inc(hi_ready, 1)
                if kind == "v":
                    act.wait_ge(side_full, job.full)
                    act.copy(v_sb[:, parity, cols], job.ps).then_inc(job.free, 1)

            def copy_head(head):
                if isinstance(head, int):
                    act.copy(h_head[:, :], hT[:, head * P:(head + 1) * P]).then_inc(head_copied, 1)
                else:
                    act.copy(h_head[:, :], hT[:, bass.ds(head * P, P)]).then_inc(head_copied, 1)

            def copy_pv(unit_done):
                act.wait_ge(pv_done, PAIRS * unit_done)
                act.copy(oT[:, :], ps[:, PV_BANK:PV_BANK + 2, :].rearrange("p a b -> p (a b)")).then_inc(o_copied, 1)

            for local, (kind, i) in enumerate(PROLOGUE):
                if kind == "peak" and i == 0:
                    for n in range(len(FIRST_SETUP), len(FIRST_SETUP + SECOND_SETUP)):
                        keep_setup(n)
                    layernorm_root(act, range(1, BLOCKS), 2)
                    act.wait_ge(shift_ln_ready, 1)
                    for b in range(1, POOL_FROM):
                        act.activation(x_mid[:, b, :], x_in[:, b, :], ACT.Identity, scale=rstd[:, b:b + 1],
                                       bias=shift_ln[:, b:b + 1]).then_inc(normed, 1)
                    act.wait_ge(mod_ready, 1)
                    act.wait_ge(w_loaded["wo"], 32)
                    act.activation(wo_nat, wo_nat, ACT.Copy, scale=mod[:, 2:3]).then_inc(folded, 1)
                    act.wait_ge(w_loaded["ffn"], 96)
                    act.activation(w2_nat, w2_nat, ACT.Copy, scale=mod[:, 5:6]).then_inc(folded, 1)
                    act.activation(sw2_nat, sw2_nat, ACT.Copy, scale=mod[:, 5:6]).then_inc(folded, 1)
                    act.activation(std[:, 0:1], eps[:, :], ACT.Exp)
                if kind == "peak" and i in setup_after:
                    for n in setup_after[i]:
                        keep_setup(n)
                if kind == "v" and i == 0:
                    act.wait_ge(kept, len(SETUP))
                side(Job(None, local), kind, i, 0, 0)

            def body(t):
                local = 0
                for p, half, head, unit, plan in units(t):
                    first = isinstance(t, int) and t == 0 and p == 0 and half == 0
                    last_head = isinstance(t, int) and t == END_T and p == 1
                    if half == 0 and not last_head:
                        copy_head(head + 1)
                    for step, places in enumerate(plan):
                        for place, jobs in enumerate(places):
                            if place < 2:
                                kt = 2 * step + place
                                act.wait_ge(scored, unit * TILES + (kt + 1))
                                if not (first and kt < PROBS):
                                    old = kt - PROBS
                                    if kt % 2 == 0:
                                        act.wait_ge(pv_done, unit * PAIRS + (old // 2 + 1))
                                    act.wait_ge(added, unit * (TILES - 1) + (adds(old % TILES)
                                                - (TILES - 1 if old < 0 else 0)))
                                act.activation(probs[:, kt % PROBS, :],
                                               ps[:, 2 * place:2 * place + 2, :].rearrange("p a b -> p (a b)"),
                                               ACT.Exp, scale=SCALE).then_inc(exped, 1)
                            for kind, i in jobs:
                                side(Job(t, local), kind, i, 1 - p, head + 1)
                                local += 1
                        if step == 0 and not first:
                            copy_pv(unit)
                        if step == 1 and last_head and half == 1:
                            layernorm_root(act, range(READY_BLOCKS), 3)

            pairs_of_heads(act, body)
            copy_pv(UNITS)
            for k, (kind, i) in enumerate(EPILOGUE):
                side(Job(END_T, LAST_LOCAL + k), kind, i, None, None)
            keep_spread(act, 0)
            keep_spread(act, 1)
            ffn_act(act)

        @block.gpsimd
        def _(pool):
            pool.memset(ident[:, :], 0.0).then_inc(consts, 1)
            pool.memset(ones[:, :], 1.0).then_inc(consts, 1)
            pool.wait_ge(consts, 2)
            pool.affine_select(out=ident[:, :], in_=ident[:, :], compare_op=ALU.not_equal, fill=1.0, base=0,
                               pattern=[[-1, P]], channel_multiplier=1).then_inc(consts, 1)
            pool.memset(eps[:, :], EPS).then_inc(consts, 1)
            pool.wait_ge(consts, 3)
            pool.memset(earlier[:, :, :], 0.0).then_inc(consts, 1)
            pool.wait_ge(consts, 5)
            for e in range(1, EXPERTS):
                pool.memset(earlier[:, e, 0:e], 1.0).then_inc(consts, 1)
            pool.wait_ge(shift_ln_ready, 1)
            for b in range(POOL_FROM, BLOCKS):
                pool.tensor_scalar(x_mid[:, b, :], x_in[:, b, :], mean_var[:, b, 0:1], rstd[:, b:b + 1],
                                   ALU.subtract, ALU.mult).then_inc(normed_pool, 1)

            def add_tile(unit, half, kt):
                pool.wait_ge(exped, unit * TILES + (kt + 1))
                total = acc[:, half, :]
                if kt > 1:
                    pool.wait_ge(added, unit * (TILES - 1) + (kt - 1))
                pool.tensor_tensor(total, total if kt > 1 else probs[:, 0, :], probs[:, kt % PROBS, :],
                                   ALU.add).then_inc(added, 1)

            def sum_head(job, head):
                pool.wait_ge(job.free, job.turn + 1)
                for k, n in enumerate((8, 4, 2, 1)):
                    pool.tensor_tensor(y_parts[:, 0:n, :], y_parts[:, 0:n, :], y_parts[:, n:2 * n, :],
                                       ALU.add).then_inc(tree, 1)
                    pool.wait_ge(tree, head * 4 + (k + 1))
                at = slice(head, head + 1) if isinstance(head, int) else bass.ds(head, 1)
                pool.tensor_tensor(x_mid[:, at, :], y_parts[:, 0:1, :], x_in[:, at, :], ALU.add).then_inc(mid_ready, 1)

            def body(t):
                local = 0
                for p, half, head, unit, plan in units(t):
                    first = isinstance(t, int) and t == 0 and p == 0 and half == 0
                    for step, places in enumerate(plan):
                        for place, jobs in enumerate(places):
                            kt = 2 * step + place
                            if 0 < kt < 2 * step + 2:
                                add_tile(unit, half, kt)
                            for kind, i in jobs:
                                if kind == "out" and i == 1 and half == 0 and not first:
                                    sum_head(Job(t, local), head - 1)
                                local += 1

            pairs_of_heads(pool, body)
            weigh_tokens(pool, 0)
            weigh_tokens(pool, 1)
            sum_head(Job(END_T, LAST_LOCAL + EPILOGUE.index(("out", 1))), HEADS - 1)
            for m in range(2, ITEMS):
                weigh_tokens(pool, m)

        @block.vector
        def _(dve):
            links = [0]

            def link(ins):
                links[0] += 1
                ins.then_inc(dve_chain, 1)
                dve.wait_ge(dve_chain, links[0])

            dve.wait_ge(cond_exp, 1)
            link(dve.tensor_scalar(cond_c[:, 2:3], cond_c[:, 1:2], 1.0, None, ALU.add))
            link(dve.reciprocal(cond_c[:, 3:4], cond_c[:, 2:3]))
            dve.tensor_tensor(cond_c[:, 1:2], cond_c[:, 0:1], cond_c[:, 3:4], ALU.mult).then_inc(mod_psum, 1)
            dve.wait_ge(first_loaded, 16)
            layernorm_stats(dve, link, x_in, range(1))
            layernorm_rstd(dve, link, range(1), 1)
            layernorm_apply(dve, x_in, x_mid, range(1))
            dve.wait_ge(consts, 2)
            dve.tensor_scalar(k_shift[SHIFT_ROW:SHIFT_ROW + 1, :, :].rearrange("p a b -> p (a b)"),
                              ones[SHIFT_ROW:SHIFT_ROW + 1, 0:1].broadcast_to([1, 2 * POSITIONS]), -1.0, None,
                              ALU.mult).then_inc(minus_one, 1)
            dve.wait_ge(mod_psum, 2)
            link(dve.tensor_copy(mod[:, :], ps[:, 5, 0:6]))
            link(dve.tensor_scalar(mod[:, 1:5:3], mod[:, 1:5:3], 1.0, None, ALU.add))
            dve.wait_ge(first_turned, 1)
            dve.tensor_scalar(h_head[:, :], ps[:, 4, 0:P], mod[:, 1:2], mod[:, 0:1],
                              ALU.mult, ALU.add).then_inc(head_copied, 1)
            gates = mod[:, 2:6:3]
            link(dve.tensor_scalar(mod_t[:, 0, :], gates, 0.0, None, ALU.is_ge))
            link(dve.tensor_scalar(mod_t[:, 1, :], mod_t[:, 0, :], 2.0, -1.0, ALU.mult, ALU.add))
            link(dve.tensor_tensor(mod_t[:, 2, :], mod_t[:, 1, :], gates, ALU.mult))
            link(dve.tensor_scalar(mod_t[:, 3, :], mod_t[:, 2, :], 0.25, None, ALU.max))
            dve.tensor_tensor(gates, mod_t[:, 3, :], mod_t[:, 1, :], ALU.mult).then_inc(mod_ready, 1)

            def side(job, kind, i, target_unit, target_half, high, parity, head_before, last_half):
                if kind in ("v", "turn", "logits", "weights"):
                    return
                dve.wait_ge(side_full, job.full)
                if kind in ("q", "k"):
                    slot = stage_of(kind, i)
                    dve.wait_ge(hi_ready, high)
                    dve.tensor_tensor(stage_lo[:, slot, :], job.ps, stage_hi[:, slot, :],
                                      ALU.subtract).then_inc(job.free, 1)
                if kind == "peak":
                    dve.tensor_reduce(peak_parts[:, i:i + 1], job.ps, AX.X, ALU.max).then_inc(job.free, 1)
                    if i == PEAKS - 1:
                        dve.wait_ge(job.free, job.turn + 1)
                        dve.wait_ge(side_free[1 - job.bank], job.turn + job.bank)
                        dve.tensor_reduce(peak[:, :], peak_parts[:, :].rearrange("p (c b) -> p c b", b=4),
                                          AX.X, ALU.max).then_inc(peak_ready, 1)
                if kind == "shift":
                    if not (isinstance(target_unit, int) and target_unit < 2):
                        dve.wait_ge(shift_ready, target_unit * 16 - 16)
                    dve.tensor_copy(shift_sb[:, target_half, :], job.ps[0:8, 0:P]).then_inc(job.free, 1)
                if kind == "sum":
                    dve.reciprocal(inv_sum[:, last_half, :], job.ps[:, 0:8]).then_inc(job.free, 1)
                    dve.wait_ge(job.free, job.turn + 1)
                if kind == "out":
                    if i == 0 and last_half == 0 and not (isinstance(head_before, int) and head_before == 0):
                        dve.wait_ge(mid_ready, head_before)
                    chunk = 8 * last_half + 4 * i
                    dve.tensor_tensor(y_parts[:, chunk:chunk + 4, :], job.ps.rearrange("p (c d) -> p c d", d=DIM),
                                      inv_sum[:, last_half, 4 * i:4 * i + 4, None].broadcast_to([P, 4, DIM]),
                                      ALU.mult).then_inc(job.free, 1)

            for local, (kind, i) in enumerate(PROLOGUE):
                if (kind, i) == ("peak", 0):
                    dve.wait_ge(x_loaded, 16)
                    layernorm_stats(dve, link, x_in, range(1, BLOCKS))
                    layernorm_rstd(dve, link, range(1, BLOCKS), 2)
                    link(dve.tensor_tensor(shift_ln[:, :], mean_var[:, :, 0], rstd[:, :], ALU.mult))
                    dve.tensor_scalar(shift_ln[:, :], shift_ln[:, :], -1.0, None, ALU.mult).then_inc(shift_ln_ready, 1)
                high = PROJECTIONS.index((kind, i)) + 1 if kind in ("q", "k") else 0
                side(Job(None, local), kind, i, 0, 0, high, 0, None, None)

            def body(t):
                local = 0
                for p, half, head, unit, plan in units(t):
                    last_unit = isinstance(t, int) and t == END_T and p == 1 and half == 1
                    if last_unit:
                        dve.wait_ge(mid_ready, READY_BLOCKS)
                        layernorm_stats(dve, link, x_mid, range(READY_BLOCKS))
                        layernorm_rstd(dve, link, range(READY_BLOCKS), 3)
                        layernorm_apply(dve, x_mid, x_in, range(READY_BLOCKS))
                        make_select(dve)
                        link(dve.memset(weight_nat, 0.0))
                    for places in plan:
                        for jobs in places:
                            for kind, i in jobs:
                                high = head * 4 + (4 + PROJECTIONS.index((kind, i)) + 1 if kind in "qk" else 0)
                                side(Job(t, local), kind, i, unit + 1, 1 - half, high, 1 - p, head - 1 + half,
                                     1 - half)
                                if kind == "logits":
                                    dve.wait_ge(consts, 5 + EXPERTS - 1)
                                    gate(dve, link, Job(t, local), 0)
                                local += 1

            pairs_of_heads(dve, body)
            for k, (kind, i) in enumerate(EPILOGUE):
                job = Job(END_T, LAST_LOCAL + k)
                side(job, kind, i, None, None, None, None, HEADS - 1, 1)
            ffn_dve(dve, link)

        @block.tensor
        def _(pe):
            def turn_weights(n):
                name, i = SETUP[n]
                if n >= SETUP_BANKS:
                    pe.wait_ge(kept, n - SETUP_BANKS + 1)
                bank = ps[:, n % SETUP_BANKS, :]
                if name in ("wq", "wk", "wv"):
                    pe.wait_ge(w_loaded[name], 16)
                    nat = {"wq": wq_nat, "wk": wk_nat, "wv": wv_nat}[name]
                    for k in range(4):
                        mm = pe.transpose(bank[:, k * P:(k + 1) * P], nat[:, (4 * i + k) * P:(4 * i + k + 1) * P],
                                          ident[:, :])
                if name == "h":
                    for k in range(1 if i == 0 else 0, 4):
                        b = 4 * i + k
                        if b < POOL_FROM:
                            pe.wait_ge(normed, b + 1)
                        else:
                            pe.wait_ge(normed_pool, b - POOL_FROM + 1)
                        mm = pe.transpose(bank[:, k * P:(k + 1) * P], x_mid[:, 4 * i + k, :], ident[:, :])
                if name == "wo":
                    pe.wait_ge(folded, 1)
                    for k in range(4):
                        mm = pe.transpose(bank[:, k * P:(k + 1) * P], wo_nat[:, 4 * i + k, :], ident[:, :])
                if name in ("w1", "w2", "w3"):
                    pe.wait_ge(w_loaded["ffn"], 96)
                    if name == "w2":
                        pe.wait_ge(folded, 3)
                    nat, shared = {"w1": (w1_nat, sw1_nat), "w2": (w2_nat, sw2_nat), "w3": (w3_nat, sw3_nat)}[name]
                    for k in range(3):
                        e = 3 * i + k
                        mm = pe.transpose(bank[:, k * P:(k + 1) * P], nat[:, e, :] if e < EXPERTS else shared,
                                          ident[:, :])
                if name == "gate":
                    pe.wait_ge(w_loaded["small"], 32)
                    pe.transpose(bank[:, 0:EXPERTS], gate_nat[:, :], ident[0:EXPERTS, 0:EXPERTS])
                    mm = pe.matmul(bank[:, EXPERTS:2 * EXPERTS], ones[0:1, :], bias_row[:, :], start=True, stop=True)
                mm.then_inc(turned, 1)

            pe.wait_ge(consts, 3)
            turn_weights(0)
            turn_weights(1)
            pe.wait_ge(normed, 1)
            pe.transpose(ps[:, 4, 0:P], x_mid[:, 0, :], ident[:, :]).then_inc(first_turned, 1)
            pe.wait_ge(mod_psum, 1)
            pe.wait_ge(wmod_loaded, 16)
            for i in range(6):
                mm = pe.matmul(ps[:, 5, i:i + 1], wmod_nat[:, i * P:(i + 1) * P], cond_c[:, 1:2], start=True, stop=True)
            mm.then_inc(mod_psum, 1)
            turn_weights(2)
            turn_weights(3)

            def side(job, kind, i, parity, target_parity, target_half, target_unit, heads_copied,
                     before_unit, last_half):
                if job.has_earlier:
                    pe.wait_ge(job.free, job.may_use)
                bank = job.ps
                if kind in ("q", "k"):
                    if kind == "q" and i == 0:
                        pe.wait_ge(head_copied, heads_copied)
                    w = wqT if kind == "q" else wkT
                    for k in range(4):
                        at = i * BANK + k * P
                        mm = pe.matmul(bank[:, k * P:(k + 1) * P], w[:, at:at + P], h_head[:, :],
                                       start=True, stop=True)
                if kind == "v":
                    mm = pe.matmul(bank, h_head[:, :], wvT[:, i * BANK:(i + 1) * BANK], start=True, stop=True)
                if kind == "peak":
                    if i == 0:
                        target_head = heads_copied - 1 - target_half
                        for which in (("q", 0), ("k", 0), ("k", 1)) if target_half == 0 else (("q", 1),):
                            pe.wait_ge(placed[stage_of(*which)], sends(*which, target_head))
                    q = target_half * HALF + (i // 4) * P
                    mm = pe.matmul(bank, q_hi[:, target_parity, q:q + P],
                                   k_hi_lo[:, target_parity, (i % 4) * BANK:(i % 4 + 1) * BANK], start=True, stop=True)
                if kind == "shift":
                    target_head = heads_copied - 1 - target_half
                    pe.wait_ge(placed_low[stage_of("q", target_half)], sends("q", target_half, target_head))
                    pe.wait_ge(peak_ready, target_unit + 1)
                    mm = pe.transpose(bank[0:8, 0:P], peak[:, :], ident[:, :])
                if kind == "sum":
                    pe.wait_ge(added, before_unit * (TILES - 1) + (TILES - 1))
                    for c in range(8):
                        mm = pe.matmul(bank[:, c:c + 1], acc[:, last_half, c * P:(c + 1) * P], ones[:, 0:1],
                                       start=True, stop=True)
                if kind == "out":
                    if i == 0:
                        pe.wait_ge(o_copied, before_unit + 1)
                    for k in range(4):
                        c = 4 * i + k
                        mm = pe.matmul(bank[:, k * P:(k + 1) * P], oT[:, c * P:(c + 1) * P],
                                       wo2[:, chunk_of(8 * last_half + c), :], start=True, stop=True)
                if kind == "turn":
                    for k in range(4):
                        pe.wait_ge(normed, POOL_FROM + 4 * i + k + 1)
                        mm = pe.transpose(bank[:, k * P:(k + 1) * P], x_in[:, 4 * i + k, :], ident[:, :])
                if kind == "logits":
                    pe.wait_ge(side_free[1 - job.bank], job.full - 1 - job.turn)
                    for k, b in enumerate(gating_blocks(i)):
                        mm = pe.matmul(bank[:, k * EXPERTS:(k + 1) * EXPERTS], hT[:, b * P:(b + 1) * P], gateT[:, :],
                                       start=True, stop=True)
                if kind == "weights":
                    pe.wait_ge(weights_ready, 1 if i < 3 else 2)
                    for k in range(4):
                        mm = pe.transpose(bank[0:LOW_ROW + EXPERTS, k * P:(k + 1) * P], weight_nat[:, 4 * i + k, :],
                                          ident[:, :])
                mm.then_inc(side_full, 1)

            def scores(p, half, head, unit, kt):
                slot = 2 * (kt % 2)
                q = half * HALF
                first = isinstance(unit, int) and unit == 0
                if not (first and kt < 2):
                    pe.wait_ge(exped, unit * TILES + (kt - 1))
                for b in range(2):
                    pe.matmul(ps[:, slot + b, :], k_hi_lo[:, p, kt * P:(kt + 1) * P],
                              q_hi[:, p, q + b * BANK:q + (b + 1) * BANK], start=True, stop=False)
                if kt == 0:
                    if half == 0:
                        for i in (0, 1):
                            pe.wait_ge(placed_low[stage_of("k", i)], sends("k", i, head))
                    pe.wait_ge(shift_ready, unit * 16 + 16)
                for b in range(2):
                    mm = pe.matmul(ps[:, slot + b, :], k_shift[:, p, kt * P:(kt + 1) * P],
                                   q_lo[:, p, q + b * BANK:q + (b + 1) * BANK], start=False, stop=True)
                mm.then_inc(scored, 1)

            def weigh(p, unit, pair, b):
                if b == 0:
                    if not (isinstance(unit, int) and unit == 0) and pair == 0:
                        pe.wait_ge(o_copied, unit)
                    pe.wait_ge(exped, unit * TILES + (2 * pair + 2))
                for k in range(2):
                    kt = 2 * pair + k
                    at = HEAD_DIM * k
                    mm = pe.matmul(ps[at:at + HEAD_DIM, PV_BANK + b, :], v_sb[:, p, chunk_of(kt) * HEAD_DIM:(chunk_of(kt) + 1) * HEAD_DIM],
                                   probs[:, kt % PROBS, b * BANK:(b + 1) * BANK],
                                   start=(pair == 0), stop=(pair == PAIRS - 1), tile_position=(0, at))
                if b == 1:
                    mm.then_inc(pv_done, 1)

            for local, (kind, i) in enumerate(PROLOGUE):
                if (kind, i) == ("q", 0):
                    pe.wait_ge(kept, 2)
                if (kind, i) == ("k", 0):
                    pe.wait_ge(kept, 4)
                if (kind, i) == ("v", 0):
                    pe.wait_ge(minus_one, 1)
                if (kind, i) == ("peak", 0):
                    for n in range(len(FIRST_SETUP), len(FIRST_SETUP + SECOND_SETUP)):
                        turn_weights(n)
                if (kind, i) == ("v", 0):
                    pe.wait_ge(kept, len(SETUP))
                side(Job(None, local), kind, i, 0, 0, 0, 0, 1, None, None)
                if kind == "peak":
                    for n in setup_after.get(i, []):
                        turn_weights(n)

            def body(t):
                local = 0
                for p, half, head, unit, plan in units(t):
                    first = isinstance(t, int) and t == 0 and p == 0 and half == 0
                    for step, places in enumerate(plan):
                        for place, jobs in enumerate(places):
                            if place < 2:
                                scores(p, half, head, unit, 2 * step + place)
                            elif step > 0:
                                weigh(p, unit, step - 1, place - 2)
                            elif not first:
                                weigh(p if half else 1 - p, unit - 1, PAIRS - 1, place - 2)
                            for kind, i in jobs:
                                side(Job(t, local), kind, i, 1 - p, p if half == 0 else 1 - p, 1 - half, unit + 1,
                                     head + 2, unit - 1, 1 - half)
                                local += 1

            pairs_of_heads(pe, body)
            for b in range(2):
                weigh(1, UNITS - 1, PAIRS - 1, b)
            for k, (kind, i) in enumerate(EPILOGUE):
                if kind == "sum":
                    spread(pe, 0)
                    spread(pe, 1)
                side(Job(END_T, LAST_LOCAL + k), kind, i, None, None, None, None, None, UNITS - 1, 1)
            ffn_pe(pe, side)


_INS = ['L0_attn_x', 'L0_attn_wq', 'L0_attn_wk', 'L0_attn_wv', 'L0_attn_wo', 'L0_ffn_gate_w', 'L0_ffn_w1',
        'L0_ffn_w2', 'L0_ffn_w3', 'L0_ffn_sw1', 'L0_ffn_sw2', 'L0_ffn_sw3', 'L0_ffn_expert_bias', 'L0_c', 'L0_wmod']
_OUTS = [((1, TOKENS, DIM), 'float32')]


def kernel(**inputs):
    import numpy as _np
    import concourse.bacc as _bacc
    from concourse import mybir as _mybir
    from concourse.bass_utils import run_bass_kernel_spmd as _run

    nc = _bacc.Bacc("TRN2", target_bir_lowering=False, num_devices=1)
    arrays, args = {}, []
    for name in _INS:
        a = _np.ascontiguousarray(inputs[name])
        arrays[f"in_{name}_dram"] = a
        args.append(nc.dram_tensor(f"in_{name}_dram", a.shape, _mybir.dt.from_np(a.dtype), kind="ExternalInput").ap())
    for i, (shape, dtype) in enumerate(_OUTS):
        dt = _mybir.dt.from_np(_np.dtype(dtype))
        args.append(nc.dram_tensor(f"out_{i}_dram", shape, dt, kind="ExternalOutput").ap())
    build(nc, *args)
    r = _run(nc, [arrays], core_ids=[0])
    got = tuple(r.results[0][f"out_{i}_dram"] for i in range(len(_OUTS)))
    return got[0]
```
